# Optimizing a Trainium2 kernel written in Bass

```python
import numpy as np
import jax
import jax.numpy as jnp

def _softmax(x, axis=-1):
    return jax.nn.softmax(x, axis=axis)

def _gelu(x):
    return jax.nn.gelu(x, approximate=True)

def _silu(x):
    return jax.nn.silu(x)

def _sigmoid(x):
    return jax.nn.sigmoid(x)

def _layernorm(x, axis=-1, eps=1e-05):
    m = jnp.mean(x, axis=axis, keepdims=True)
    v = jnp.var(x, axis=axis, keepdims=True)
    return (x - m) / jnp.sqrt(v + eps)

def _scatter_add(tgt, idx, src, axis=0):
    return tgt.at[idx].add(src)

def _segment_sum(src, seg, n):
    return jax.ops.segment_sum(src, seg, n)
kernel_name = 'mk_macaron_d1_jaxref_r4_64ac9c'

def setup_inputs(seed: int=0):
    np.random.seed(seed)
    _w = jnp.asarray

    def _L0_attn_setup():
        import jax, jax.numpy as jnp
        import numpy as np
        N_HEADS = 32
        WINDOW = 128

        def _sliding_window_attention(x, Wq, Wk, Wv, Wo, n_heads=N_HEADS, window=WINDOW):
            B, T, D = x.shape
            H, dk = (n_heads, D // n_heads)
            bs = window
            assert T % bs == 0
            nb = T // bs

            def heads(y):
                return y.reshape(B, T, H, dk).transpose(0, 2, 1, 3)
            q = heads(x @ Wq.T)
            k = heads(x @ Wk.T)
            v = heads(x @ Wv.T)
            qb = q.reshape(B, H, nb, bs, dk)
            zpad = jnp.zeros((B, H, bs, dk), dtype=x.dtype)
            kp = jnp.concatenate([zpad, k], axis=2).reshape(B, H, nb + 1, bs, dk)
            vp = jnp.concatenate([zpad, v], axis=2).reshape(B, H, nb + 1, bs, dk)
            kw = jnp.concatenate([kp[:, :, :-1], kp[:, :, 1:]], axis=3)
            vw = jnp.concatenate([vp[:, :, :-1], vp[:, :, 1:]], axis=3)
            scale = 1.0 / np.sqrt(dk).astype(np.float32)
            scores = jnp.einsum('bhnrd,bhncd->bhnrc', qb, kw) * scale
            i = jnp.arange(nb)[:, None, None]
            r = jnp.arange(bs)[None, :, None]
            c = jnp.arange(2 * bs)[None, None, :]
            dist = bs + r - c
            key_global = i * bs - bs + c
            valid = (dist >= 0) & (dist <= window) & (key_global >= 0)
            scores = jnp.where(valid[None, None], scores, jnp.finfo(scores.dtype).min)
            probs = jax.nn.softmax(scores, axis=-1)
            out = jnp.einsum('bhnrc,bhncd->bhnrd', probs, vw)
            out = out.reshape(B, H, T, dk).transpose(0, 2, 1, 3).reshape(B, T, D)
            return out @ Wo.T
        key = jax.random.key(seed)
        ks = jax.random.split(key, 5)
        B, T, D = (2, 1024, 512)
        w_std = 0.02
        return {'x': jax.random.normal(ks[0], (B, T, D), dtype=jnp.float32), 'Wq': jax.random.normal(ks[1], (D, D), dtype=jnp.float32) * w_std, 'Wk': jax.random.normal(ks[2], (D, D), dtype=jnp.float32) * w_std, 'Wv': jax.random.normal(ks[3], (D, D), dtype=jnp.float32) * w_std, 'Wo': jax.random.normal(ks[4], (D, D), dtype=jnp.float32) * w_std}
    _L0_attn_in = _L0_attn_setup()

    def _L0_ffn_setup():
        import jax, jax.numpy as jnp
        import numpy as np
        GROUP_SIZE = 64

        def ternary_quant(w_fp32, g=GROUP_SIZE):
            w = w_fp32.astype(jnp.bfloat16)
            w_g = w.reshape(-1, g)
            scale = jnp.clip(jnp.mean(jnp.abs(w_g), axis=-1, keepdims=True), 1e-08, None)
            q = jnp.clip(jnp.round(w_g / scale), -1, 1)
            w_hat = (q * scale).reshape(w.shape)
            return w + jax.lax.stop_gradient(w_hat - w)

        def rms_norm(x):
            eps = jnp.finfo(x.dtype).eps.astype(jnp.float32)
            xf = x.astype(jnp.float32)
            inv = jax.lax.rsqrt(jnp.mean(xf * xf, axis=-1, keepdims=True) + eps)
            return (xf * inv).astype(x.dtype)
        key = jax.random.key(seed)
        k1, k2, k3 = jax.random.split(key, 3)
        B, S, D = (2, 512, 512)
        H = 4 * D
        x = jax.random.normal(k1, (B, S, D), dtype=jnp.float32).astype(jnp.bfloat16)
        w_gate_up = jax.random.normal(k2, (2 * H, D), dtype=jnp.float32) * 0.02
        w_proj = jax.random.normal(k3, (D, H), dtype=jnp.float32) * 0.02
        return {'x': x, 'w_gate_up': w_gate_up, 'w_proj': w_proj}
    _L0_ffn_in = _L0_ffn_setup()
    _d = {'L0_attn_x': _L0_attn_in['x'], 'L0_attn_Wq': _L0_attn_in['Wq'], 'L0_attn_Wk': _L0_attn_in['Wk'], 'L0_attn_Wv': _L0_attn_in['Wv'], 'L0_attn_Wo': _L0_attn_in['Wo'], 'L0_ffn_w_gate_up': _L0_ffn_in['w_gate_up'], 'L0_ffn_w_proj': _L0_ffn_in['w_proj']}
    _x0 = _d['L0_attn_x']
    _d['L0_attn_x'] = jax.random.normal(jax.random.fold_in(jax.random.key(seed), 1), (8, 512, 512), dtype=_x0.dtype)
    del _x0
    return _d

def reference(L0_attn_x, L0_attn_Wq, L0_attn_Wk, L0_attn_Wv, L0_attn_Wo, L0_ffn_w_gate_up, L0_ffn_w_proj):

    def _L0_attn_ref(x, Wq, Wk, Wv, Wo):
        import jax, jax.numpy as jnp
        import numpy as np
        N_HEADS = 32
        WINDOW = 128

        def _sliding_window_attention(x, Wq, Wk, Wv, Wo, n_heads=N_HEADS, window=WINDOW):
            B, T, D = x.shape
            H, dk = (n_heads, D // n_heads)
            bs = window
            assert T % bs == 0
            nb = T // bs

            def heads(y):
                return y.reshape(B, T, H, dk).transpose(0, 2, 1, 3)
            q = heads(x @ Wq.T)
            k = heads(x @ Wk.T)
            v = heads(x @ Wv.T)
            qb = q.reshape(B, H, nb, bs, dk)
            zpad = jnp.zeros((B, H, bs, dk), dtype=x.dtype)
            kp = jnp.concatenate([zpad, k], axis=2).reshape(B, H, nb + 1, bs, dk)
            vp = jnp.concatenate([zpad, v], axis=2).reshape(B, H, nb + 1, bs, dk)
            kw = jnp.concatenate([kp[:, :, :-1], kp[:, :, 1:]], axis=3)
            vw = jnp.concatenate([vp[:, :, :-1], vp[:, :, 1:]], axis=3)
            scale = 1.0 / np.sqrt(dk).astype(np.float32)
            scores = jnp.einsum('bhnrd,bhncd->bhnrc', qb, kw) * scale
            i = jnp.arange(nb)[:, None, None]
            r = jnp.arange(bs)[None, :, None]
            c = jnp.arange(2 * bs)[None, None, :]
            dist = bs + r - c
            key_global = i * bs - bs + c
            valid = (dist >= 0) & (dist <= window) & (key_global >= 0)
            scores = jnp.where(valid[None, None], scores, jnp.finfo(scores.dtype).min)
            probs = jax.nn.softmax(scores, axis=-1)
            out = jnp.einsum('bhnrc,bhncd->bhnrd', probs, vw)
            out = out.reshape(B, H, T, dk).transpose(0, 2, 1, 3).reshape(B, T, D)
            return out @ Wo.T
        return _sliding_window_attention(x, Wq, Wk, Wv, Wo)

    def _L0_ffn_ref(x, w_gate_up, w_proj):
        import jax, jax.numpy as jnp
        import numpy as np
        GROUP_SIZE = 64

        def ternary_quant(w_fp32, g=GROUP_SIZE):
            w = w_fp32.astype(jnp.bfloat16)
            w_g = w.reshape(-1, g)
            scale = jnp.clip(jnp.mean(jnp.abs(w_g), axis=-1, keepdims=True), 1e-08, None)
            q = jnp.clip(jnp.round(w_g / scale), -1, 1)
            w_hat = (q * scale).reshape(w.shape)
            return w + jax.lax.stop_gradient(w_hat - w)

        def rms_norm(x):
            eps = jnp.finfo(x.dtype).eps.astype(jnp.float32)
            xf = x.astype(jnp.float32)
            inv = jax.lax.rsqrt(jnp.mean(xf * xf, axis=-1, keepdims=True) + eps)
            return (xf * inv).astype(x.dtype)
        wq_gu = ternary_quant(w_gate_up)
        gu = jnp.einsum('bsd,hd->bsh', x, wq_gu)
        gate, up = jnp.split(gu, 2, axis=-1)
        h = jax.nn.silu(gate) * up
        hn = rms_norm(h)
        wq_p = ternary_quant(w_proj)
        return jnp.einsum('bsh,dh->bsd', hn, wq_p)
    x = L0_attn_x
    x = x + 0.5 * _L0_ffn_ref(_layernorm(x, axis=-1), L0_ffn_w_gate_up, L0_ffn_w_proj)
    x = x + _L0_attn_ref(_layernorm(x, axis=-1), L0_attn_Wq, L0_attn_Wk, L0_attn_Wv, L0_attn_Wo)
    x = x + 0.5 * _L0_ffn_ref(_layernorm(x, axis=-1), L0_ffn_w_gate_up, L0_ffn_w_proj)
    return x

_drawn_inputs = setup_inputs


def setup_inputs(seed=0):
    import zlib

    import numpy as np

    out = dict(_drawn_inputs(seed))
    spreads = {}
    factors = {'L0_attn_Wq': 8.0, 'L0_attn_Wk': 8.0}
    for name, (base, spread) in spreads.items():
        noise = np.random.default_rng([zlib.crc32(name.encode()), seed]).standard_normal(out[name].shape)
        drawn = base * np.exp(spread * noise) if base else spread * noise
        out[name] = jnp.asarray(drawn.astype(out[name].dtype))
    for name, factor in factors.items():
        out[name] = (out[name] * factor).astype(out[name].dtype)
    return out
```

```python
from contextlib import ExitStack
import math

import concourse.bass as bass
from concourse import mybir

F32 = mybir.dt.float32
F16 = mybir.dt.float16
BF16 = mybir.dt.bfloat16
U32 = mybir.dt.uint32
ALU = mybir.AluOpType
ACT = mybir.ActivationFunctionType
AX = mybir.AxisListType
RMAX = bass.bass_isa.ReduceOp.max

P = 128
HEADS = 32
LN_EPS = 1e-5
RMS_EPS = 2.0 ** -23
CLIP_MIN = 1.0011717677116394e-08
NEG = -3.0e38
PROB_LOG2 = 15


def macaron(nc, x, Wq, Wk, Wv, Wo, w_gate_up, w_proj, out):
    B, S, D = x.shape
    H = w_proj.shape[1]
    KD, KH = D // P, H // P
    DK = D // HEADS
    NB = B * S // P
    BPS = S // P
    CH = 512
    NC = H // CH
    XS_LOG2 = 11
    WS_LOG2 = 13
    DOWN_LOG2 = XS_LOG2 + WS_LOG2 - 5
    HS_LOG2 = 10
    RING = 7
    assert D == 512 and H == 2048 and DK == 16 and NC == 4

    xf = x.rearrange("b t d -> (b t) d")
    of = out.rearrange("b t d -> (b t) d")
    gu_units = w_gate_up.rearrange("(u t p) d -> u p t d", t=4, p=P)
    wp_units = w_proj.rearrange("(u p) h -> u p h", p=P)
    at_units = [w.rearrange("(t p) d -> p t d", p=P) for w in (Wq, Wk, Wv, Wo)]
    NGU, NWP = 2 * H // 512, D // P
    NTU = NGU + NWP
    G64 = 32

    with ExitStack() as ctx:
        def sb(name, shape, dt):
            return ctx.enter_context(nc.sbuf_tensor(name, shape, dt))

        def psum(name, shape):
            return ctx.enter_context(nc.psum_tensor(name, shape, F32))

        def sem(name):
            return ctx.enter_context(nc.semaphore(name))

        ps_s = psum("ps_s", [P, 1024])
        ps_gu = psum("ps_gu", [P, 1024])
        ps_y = psum("ps_y", [P, CH])
        ps_ht = psum("ps_ht", [P, CH])
        ps_o = psum("ps_o", [P, CH])
        ps_m = psum("ps_m", [P, CH])
        ps_m16 = ps_m[:, :].bitcast(F16).rearrange("p (a b) -> p a b", b=P)

        wgu_t = sb("wgu_t", [P, KD, 2 * H], BF16)
        wp_t = sb("wp_t", [P, KH, D], BF16)
        wat_hi = [sb(f"w{n}_hi", [P, KD, D], F16) for n in "qkvo"]
        wat_lo = [sb(f"w{n}_lo", [P, KD, D], F16) for n in "qkvo"]
        Q, K, V, O = range(4)
        stream = sb("stream", [P, RING, D], F32)
        xhat = sb("xhat", [P, D], F32)
        xt_hi = {s: sb(f"xt_hi_{s}", [P, KD, P], F16) for s in "ABC"}
        xt_lo = {s: sb(f"xt_lo_{s}", [P, KD, P], F16) for s in "ABC"}
        gate = sb("gate", [P, 2, CH], F32)
        h = {s: sb(f"h_{s}", [P, H], F32) for s in "AC"}
        ht_hi = sb("ht_hi", [P, 2, 4, P], F16)
        ht_lo = sb("ht_lo", [P, 2, 4, P], F16)
        qk4 = sb("qk4", [P, HEADS, 4, DK], F16)
        qt_next = sb("qt_next", [P, HEADS // 2, P], F16)
        kt_next = sb("kt_next", [P, HEADS // 2, P], F16)
        qt = sb("qt", [P, HEADS // 2, P], F16)
        kt = sb("kt", [P, HEADS // 2, 2 * P], F16)
        v_next = sb("v_next", [P, HEADS, 3, DK], BF16)
        v_cur = sb("v_cur", [P, HEADS, 3, DK], BF16)
        v_prev = sb("v_prev", [P, HEADS, 3, DK], BF16)
        prob = sb("prob", [P, 2, 8, 2 * P], F32)
        pt_hi = sb("pt_hi", [P, 8, P], F16)
        pt_lo = sb("pt_lo", [P, 8, P], F16)
        o_sum = sb("o_sum", [P, 8, DK], F32)
        o_norm = sb("o_norm", [P, D], F32)
        ot_hi = sb("ot_hi", [P, KD, P], F16)
        ot_lo = sb("ot_lo", [P, KD, P], F16)
        id32 = sb("id32", [P, P], F32)
        id16 = sb("id16", [P, P], F16)
        idb = sb("idb", [P, P], BF16)
        mask_table = sb("mask_table", [P, BPS, P], F32)
        mask = sb("mask", [P, 2 * P], F32)
        zeros = sb("zeros", [P, P], F32)
        neg_half = sb("neg_half", [P, 1], F32)
        carrier = sb("carrier", [1, 384], F32)
        row_max = sb("row_max", [P, HEADS], F32)
        exp_bias = sb("exp_bias", [P, HEADS], F32)
        row_sum = sb("row_sum", [P, HEADS], F32)
        row_inv = sb("row_inv", [P, 8], F32)
        st6 = {s: sb(f"st6_{s}", [P, 6], F32) for s in "ABC"}
        mean_var = {s: sb(f"mean_var_{s}", [P, 2], F32) for s in "ABC"}
        var_eps = {s: sb(f"var_eps_{s}", [P, 1], F32) for s in "ABC"}
        rstd = {s: sb(f"rstd_{s}", [P, 1], F32) for s in "ABC"}
        sq_parts = {s: sb(f"sq_parts_{s}", [P, NC], F32) for s in "AC"}
        sq_sum = {s: sb(f"sq_sum_{s}", [P, 1], F32) for s in "AC"}
        sq_mean = {s: sb(f"sq_mean_{s}", [P, 1], F32) for s in "AC"}
        rms_inv = {s: sb(f"rms_inv_{s}", [P, 1], F32) for s in "AC"}
        w_absmax = sb("w_absmax", [P, 4], F32)
        w_max = sb("w_max", [P, 4], F32)
        w_floor = sb("w_floor", [P, 4], F32)
        w_pow2 = sb("w_pow2", [P, 4], F32)
        w_rec = sb("w_rec", [P, 4], F32)
        w_scale = sb("w_scale", [P, 4], F32)
        out_scale = sb("out_scale", [P, 1], F32)
        exp_scale = sb("exp_scale", [P, 1], F32)
        neg_exp_scale = sb("neg_exp_scale", [P, 1], F32)
        grp_sum = sb("grp_sum", [P, 2, G64], F32)
        grp_scale = sb("grp_scale", [P, 2, G64], BF16)
        prob_4k = [prob[:, n // 2, n % 2 * 4:n % 2 * 4 + 4, :].rearrange("p a b -> p (a b)") for n in range(4)]
        kt_4k = [kt[:, n * 8:n * 8 + 8, :].rearrange("p a b -> p (a b)") for n in range(2)]
        gate_4k = gate[:, :, :].rearrange("p a b -> p (a b)")
        qt_4k = qt[:, :, :].rearrange("p a b -> p (a b)")
        w_raw = [h["A"], h["C"]]
        w_abs = [b.bitcast(BF16) for b in prob_4k[0:3]]
        w_sign = [b.bitcast(BF16) for b in (prob_4k[3], gate_4k, qt_4k)]
        w_diff = [qk4[:, :, :, :].rearrange("p a b c -> p (a b c)").bitcast(BF16),
                  qt_next[:, :, :].rearrange("p a b -> p (a b)").bitcast(BF16)]
        w_keep = kt_next[:, :, :].rearrange("p a b -> p (a b)").bitcast(BF16)
        w_tern = [b.bitcast(BF16) for b in kt_4k]
        at_raw = [stream[:, 2:6, :], h["C"][:, :].rearrange("p (t d) -> p t d", t=4),
                  prob[:, 0, :, :].rearrange("p (t a) b -> p t (a b)", t=4),
                  prob[:, 1, :, :].rearrange("p (t a) b -> p t (a b)", t=4)]
        ps_w = [ps_s, ps_gu]

        consts = sem("consts")
        ids = sem("ids")
        w_in = [sem(f"w_in{n}") for n in (0, 1)]
        w_parts = sem("w_parts")
        w_sum = sem("w_sum")
        w_grp = sem("w_grp")
        w_dif = sem("w_dif")
        w_kp = sem("w_kp")
        w_step = sem("w_step")
        w_q = sem("w_q")
        w_tr = sem("w_tr")
        w_st = sem("w_st")
        a_in = [sem(f"a_in{m}") for m in range(4)]
        a_mx = sem("a_mx")
        a_all = sem("a_all")
        sc_step = sem("sc_step")
        a_tr = sem("a_tr")
        a_hi = sem("a_hi")
        a_lo = sem("a_lo")
        zeroed = sem("zeroed")
        p_xt = {s: sem(f"p_xt_{s}") for s in "ABC"}
        p_up = {s: sem(f"p_up_{s}") for s in "AC"}
        p_ht = {s: sem(f"p_ht_{s}") for s in "AC"}
        p_dn = {s: sem(f"p_dn_{s}") for s in "AC"}
        p_q, p_k, p_v = sem("p_q"), sem("p_k"), sem("p_v")
        p_qt, p_kt = sem("p_qt"), sem("p_kt")
        p_s = sem("p_s")
        p_pt = sem("p_pt")
        p_pv = sem("p_pv")
        p_ot, p_wo = sem("p_ot"), sem("p_wo")
        a_xt = {s: sem(f"a_xt_{s}") for s in "ABC"}
        a_tanh = {s: sem(f"a_tanh_{s}") for s in "AC"}
        a_sq = {s: sem(f"a_sq_{s}") for s in "AC"}
        a_ht = {s: sem(f"a_ht_{s}") for s in "AC"}
        a_q, a_k, a_v = sem("a_q"), sem("a_k"), sem("a_v")
        a_kt = sem("a_kt")
        a_exp = sem("a_exp")
        a_pt = sem("a_pt")
        a_ot = sem("a_ot")
        d_xt = {s: sem(f"d_xt_{s}") for s in "ABC"}
        d_gate = {s: sem(f"d_gate_{s}") for s in "AC"}
        d_h = {s: sem(f"d_h_{s}") for s in "AC"}
        d_sqs = {s: sem(f"d_sqs_{s}") for s in "AC"}
        d_sqm = {s: sem(f"d_sqm_{s}") for s in "AC"}
        d_hn = {s: sem(f"d_hn_{s}") for s in "AC"}
        d_ht = {s: sem(f"d_ht_{s}") for s in "AC"}
        d_qlo, d_klo = sem("d_qlo"), sem("d_klo")
        d_q, d_k, d_v = sem("d_q"), sem("d_k"), sem("d_v")
        d_qt = sem("d_qt")
        d_kold, d_vold = sem("d_kold"), sem("d_vold")
        d_kshift, d_vshift = sem("d_kshift"), sem("d_vshift")
        d_mx = sem("d_mx")
        d_bias = sem("d_bias")
        d_pt = sem("d_pt")
        d_ot = sem("d_ot")
        d_osum, d_rinv = sem("d_osum"), sem("d_rinv")
        d_on = sem("d_on")
        d_x1, d_x2, d_x3 = sem("d_x1"), sem("d_x2"), sem("d_x3")
        d_st = {s: sem(f"d_st_{s}") for s in "ABC"}
        d_mv = {s: sem(f"d_mv_{s}") for s in "ABC"}
        d_ve = {s: sem(f"d_ve_{s}") for s in "ABC"}
        d_xh = {s: sem(f"d_xh_{s}") for s in "ABC"}
        g_rstd = {s: sem(f"g_rstd_{s}") for s in "ABC"}
        g_rms = {s: sem(f"g_rms_{s}") for s in "AC"}
        g_vm, g_v = sem("g_vm"), sem("g_v")
        g_hold = sem("g_hold")
        g_mask = sem("g_mask")
        x_in = sem("x_in")
        x_out = sem("x_out")

        NCONST = 9

        def need(eng, s, n):
            if not isinstance(n, int) or n > 0:
                eng.wait_ge(s, n)

        def last(b):
            return min(b, NB - 1) if isinstance(b, int) else b

        places = iter(range(384))

        def place_of_carrier():
            n = next(places)
            return carrier[0:1, n:n + 1]

        def on(b):
            return not isinstance(b, int) or 0 <= b < NB

        def slot(b):
            if isinstance(b, int):
                return stream[:, b % RING, :]
            return stream[:, bass.ds((b + RING) % RING, 1), :].rearrange("p a d -> p (a d)")

        STEADY, LAST, END = 5, NB - 2, NB + 4

        def ternary_done(eng):
            eng.wait_ge(w_st, NTU)

        def attention_weights_done(eng):
            eng.wait_ge(a_hi, 8)
            eng.wait_ge(a_lo, 8)
            eng.wait_ge(sc_step, 7)
            eng.wait_ge(zeroed, 2)

        def all_iterations(eng, body, ternary_weights):
            body(-1)
            ternary_weights()
            ternary_done(eng)
            body(0)
            attention_weights_done(eng)
            for i in range(1, STEADY):
                body(i)
            with eng.Fori(STEADY, LAST + 1) as i:
                body(i)
            for i in range(LAST + 1, END):
                body(i)

        block = ctx.enter_context(nc.Block())

        @block.sync
        def _(sp):
            def ternary_weights():
                for u in range(NTU):
                    need(sp, w_parts, u - 1)
                    if u < NGU:
                        sp.dma_start(w_raw[u % 2][:, :].rearrange("p (t d) -> p t d", t=4),
                                     gu_units[u]).then_inc(w_in[u % 2], 16)
                    else:
                        sp.dma_start(w_raw[u % 2][:, :], wp_units[u - NGU]).then_inc(w_in[u % 2], 16)
                sp.dma_start(at_raw[Q], at_units[Q]).then_inc(a_in[Q], 16)
                sp.wait_ge(w_parts, NTU)
                sp.dma_start(at_raw[K], at_units[K]).then_inc(a_in[K], 16)
                sp.wait_ge(w_q, NTU)
                sp.dma_start(at_raw[V], at_units[V]).then_inc(a_in[V], 16)
                sp.dma_start(at_raw[O], at_units[O]).then_inc(a_in[O], 16)

            def body(i):
                b = i + 1
                if on(b):
                    need(sp, x_out, 16 * (b - 5))
                    need(sp, x_in, 16 * b)
                    rows = slice(b * P, (b + 1) * P) if isinstance(b, int) else bass.ds(b * P, P)
                    sp.dma_start(slot(b), xf[rows, :]).then_inc(x_in, 16)
                b = i - 4
                if on(b):
                    sp.wait_ge(d_x3, b + 1)
                    rows = slice(b * P, (b + 1) * P) if isinstance(b, int) else bass.ds(b * P, P)
                    sp.dma_start(of[rows, :], slot(b)).then_inc(x_out, 16)

            all_iterations(sp, body, ternary_weights)
            sp.wait_ge(x_out, 16 * NB)

        @block.gpsimd
        def _(pool):
            pool.memset(id32[:, :], 0.0).then_inc(consts, 1)
            pool.memset(mask_table[:, :, :], 0.0).then_inc(consts, 1)
            pool.memset(mask[:, :], 0.0).then_inc(consts, 1)
            pool.memset(zeros[:, :], 0.0).then_inc(consts, 1)
            pool.memset(neg_half[:, :], -0.5).then_inc(consts, 1)
            pool.wait_ge(consts, 5)
            pool.affine_select(out=id32[:, :], in_=id32[:, :], compare_op=ALU.not_equal, fill=1.0, base=0,
                               pattern=[[-1, P]], channel_multiplier=1).then_inc(consts, 1)
            later = mask_table[:, 1:BPS, :]
            pool.affine_select(out=later, in_=later, compare_op=ALU.is_ge, fill=NEG, base=0,
                               pattern=[[0, BPS - 1], [1, P]], channel_multiplier=-1).then_inc(consts, 1)
            pool.memset(mask_table[:, 0, :], NEG).then_inc(consts, 1)
            pool.affine_select(out=mask[:, P:2 * P], in_=mask[:, P:2 * P], compare_op=ALU.is_ge, fill=NEG, base=0,
                               pattern=[[-1, P]], channel_multiplier=1).then_inc(consts, 1)

            def ternary_weights():
                for u in range(NTU):
                    pool.wait_ge(w_grp, u + 1)
                    need(pool, w_q, u - 1)
                    pool.tensor_tensor(out=w_diff[u % 2].rearrange("p (g k) -> p g k", g=G64),
                                       in0=grp_scale[:, u % 2, :].unsqueeze(2).to_broadcast([P, G64, 64]),
                                       in1=w_abs[u % 3].rearrange("p (g k) -> p g k", g=G64),
                                       op=ALU.subtract).then_inc(w_dif, 1)

            pool.wait_ge(consts, NCONST)

            def power(s, dst, src, ready, done, b):
                pool.wait_ge(ready, b + 1)
                pool.tensor_tensor(out=dst[:, :], in0=src[:, :], in1=neg_half[:, :], op=ALU.pow).then_inc(done, 1)

            def body(i):
                if isinstance(i, int) and i == 0:
                    pool.wait_ge(a_mx, 4)
                    pool.partition_all_reduce(w_max[:, :], w_absmax[:, :], P, RMAX).then_inc(a_all, 1)
                if on(i - 1):
                    power("B", rstd["B"], var_eps["B"], d_ve["B"], g_rstd["B"], i - 1)
                if on(i - 3):
                    power("C", rstd["C"], var_eps["C"], d_ve["C"], g_rstd["C"], i - 3)
                if on(i):
                    power("A", rms_inv["A"], sq_mean["A"], d_sqm["A"], g_rms["A"], i)
                if on(i + 1):
                    power("A", rstd["A"], var_eps["A"], d_ve["A"], g_rstd["A"], i + 1)
                if on(i - 1):
                    b = i - 1
                    need(pool, d_bias, 8 * b)
                    pool.tensor_tensor(out=place_of_carrier(), in0=zeros[0:1, 0:1], in1=zeros[0:1, 1:2],
                                       op=ALU.add).then_inc(g_hold, 1)
                    place = (mask_table[:, b % BPS, :] if isinstance(b, int) else
                             mask_table[:, bass.ds((b + BPS) % BPS, 1), :].rearrange("p a d -> p (a d)"))
                    pool.tensor_tensor(out=mask[:, 0:P], in0=place, in1=zeros[:, :], op=ALU.add).then_inc(g_mask, 1)
                if on(i - 3):
                    power("C", rms_inv["C"], sq_mean["C"], d_sqm["C"], g_rms["C"], i - 3)
                if on(i - 1):
                    b = i - 1
                    pool.wait_ge(d_v, b + 1)
                    vr = xhat[:, :].rearrange("p (h d) -> p h d", d=DK)
                    pool.tensor_tensor(out=v_next[:, :, 1, :], in0=vr,
                                       in1=zeros[:, 0:1].unsqueeze(2).to_broadcast([P, HEADS, DK]),
                                       op=ALU.add).then_inc(g_vm, 1)
                    pool.wait_ge(g_vm, b + 1)
                    pool.tensor_tensor(out=v_next[:, :, 2, :], in0=vr, in1=v_next[:, :, 1, :],
                                       op=ALU.subtract).then_inc(g_v, 1)

            all_iterations(pool, body, ternary_weights)

        @block.scalar
        def _(act):
            def ternary_weights():
                def parts(u):
                    act.wait_ge(w_in[u % 2], 16 * (u // 2 + 1))
                    need(act, w_q, u - 2)
                    act.activation(w_abs[u % 3], w_raw[u % 2][:, :], ACT.Abs)
                    act.activation(w_sign[u % 3], w_raw[u % 2][:, :], ACT.Sign).then_inc(w_parts, 1)

                def store(u):
                    act.wait_ge(w_tr, u + 1)
                    dst = (wgu_t[:, :, u * 512:(u + 1) * 512] if u < NGU else
                           wp_t[:, :, (u - NGU) * P:(u - NGU + 1) * P])
                    act.activation(dst, ps_w[u % 2][:, :].bitcast(BF16).rearrange("p (a b) -> p a b", a=dst.shape[1]),
                                   ACT.Copy).then_inc(w_st, 1)

                for u in range(NTU + 2):
                    if u < NTU:
                        parts(u)
                    if u >= 2:
                        store(u - 2)

            def attention_weight(m):
                act.wait_ge(a_tr, m + 1)
                act.wait_ge(sc_step, 7)
                for half in (0, 1):
                    act.activation(wat_hi[m][:, 2 * half:2 * half + 2, :],
                                   ps_w[half][:, :].rearrange("p (k d) -> p k d", k=2), ACT.Copy,
                                   scale=w_scale[:, m:m + 1]).then_inc(a_hi, 1)

            def copy_hi(dst, src, ready, n, done, scale=1.0):
                act.wait_ge(ready, n)
                act.activation(dst, src, ACT.Copy, scale=scale).then_inc(done, 1)

            def xt_piece(s, b):
                copy_hi(xt_hi[s][:, :, :].rearrange("p a b -> p (a b)"), ps_m[:, :], p_xt[s], b + 1, a_xt[s])

            def half_tanh(s, b, c, n):
                act.wait_ge(p_up[s], 8 * b + 2 * c + 1)
                act.activation(gate[:, n, :], ps_gu[:, 0:CH], ACT.Tanh, scale=0.5 * 2.0 ** -XS_LOG2)\
                   .then_inc(a_tanh[s], 1)

            def square(s, b, c, n):
                act.wait_ge(d_h[s], 4 * b + c + 1)
                act.activation(gate[:, n, :], h[s][:, c * CH:(c + 1) * CH], ACT.Square,
                               accum_out=sq_parts[s][:, c:c + 1]).then_inc(a_sq[s], 1)

            def exps(b, q):
                act.wait_ge(d_bias, 8 * b + q + 1)
                for j in range(4):
                    hd = 4 * q + j
                    p = prob[:, (q // 2) % 2, hd % 8, :]
                    e = act.activation(p, p, ACT.Exp, bias=exp_bias[:, hd:hd + 1], scale=exp_scale[:, 0:1],
                                       accum_out=row_sum[:, hd:hd + 1])
                e.then_inc(a_exp, 1)

            def head_view(ap):
                return ap.rearrange("p (h d) -> p h d", d=DK)

            def body(i):
                bL, bA, bQ, bT, bW, bE = i + 1, i, i - 1, i - 2, i - 3, i - 4
                for hs in range(8):
                    up, bu = ("A", bA) if hs < 4 else ("C", bW)
                    dn, bd = ("C", bE) if hs < 4 else ("A", bA)
                    c = hs % 4
                    bp, qp = (bW, 7) if hs < 1 else (bT, hs - 1)
                    if isinstance(i, int) and i == 0 and hs >= 5:
                        attention_weight(hs - 5)
                    if on(bp):
                        exps(bp, qp)
                    if hs == 1 and on(bQ):
                        act.wait_ge(p_q, bQ + 1)
                        act.activation(qk4[:, :, 0, :], head_view(ps_m[:, :]), ACT.Copy,
                                       scale=2.0 ** -DOWN_LOG2).then_inc(a_q, 1)
                    if hs == 4 and on(bQ):
                        act.wait_ge(p_k, bQ + 1)
                        act.activation(qk4[:, :, 0, :], head_view(ps_m[:, :]), ACT.Copy,
                                       scale=2.0 ** -DOWN_LOG2).then_inc(a_k, 1)
                    if hs == 5 and on(bQ):
                        copy_hi(kt_next[:, 8:16, :], ps_m16, p_kt, 2 * bQ + 2, a_kt)
                    if on(bu):
                        half_tanh(up, bu, c, hs % 2)
                    if on(bd):
                        copy_hi(ht_hi[:, c % 2, :, :].rearrange("p a b -> p (a b)"), ps_ht[:, :],
                                p_ht[dn], 4 * bd + c + 1, a_ht[dn])
                    if hs == 0 and on(bQ):
                        xt_piece("B", bQ)
                    if hs == 2 and on(bW):
                        copy_hi(ot_hi[:, :, :].rearrange("p a b -> p (a b)"), ps_m[:, :], p_ot, bW + 1, a_ot)
                    if hs == 3 and on(bW):
                        xt_piece("C", bW)
                    if on(bp):
                        copy_hi(pt_hi[:, :, :].rearrange("p a b -> p (a b)"), ps_s[:, :], p_pt, 8 * bp + qp + 1, a_pt)
                    if hs == 4 and on(bQ):
                        need(act, d_kshift, bQ)
                        copy_hi(kt_next[:, 0:8, :], ps_m16, p_kt, 2 * bQ + 1, a_kt)
                    if hs == 6 and on(bL):
                        xt_piece("A", bL)
                    if on(bu):
                        square(up, bu, c, hs % 2)
                    if hs == 7 and on(bQ):
                        act.wait_ge(p_v, bQ + 1)
                        need(act, d_vshift, bQ)
                        act.activation(v_next[:, :, 0, :], head_view(ps_m[:, :]), ACT.Copy,
                                       scale=2.0 ** -DOWN_LOG2).then_inc(a_v, 1)
                if isinstance(i, int) and i == 0:
                    attention_weight(3)

            all_iterations(act, body, ternary_weights)

        @block.vector
        def _(dve):
            def hold():
                dve.memset(place_of_carrier(), 0.0)

            dve.wait_ge(consts, NCONST)
            dve.tensor_copy(id16[:, :], id32[:, :]).then_inc(ids, 1)
            dve.tensor_copy(idb[:, :], id32[:, :]).then_inc(ids, 1)

            def ternary_weights():
                def scales(u):
                    n = u % 2
                    dve.wait_ge(w_parts, u + 1)
                    dve.tensor_reduce(grp_sum[:, n, :], w_abs[u % 3].rearrange("p (g k) -> p g k", g=G64), AX.X,
                                      ALU.add).then_inc(w_sum, 1)
                    dve.wait_ge(w_sum, u + 1)
                    need(dve, w_dif, u - 1)
                    dve.tensor_scalar(grp_scale[:, n, :], grp_sum[:, n, :], 1.0 / 64, CLIP_MIN,
                                      ALU.mult, ALU.max).then_inc(w_grp, 1)

                def quantise(u):
                    n, m = u % 2, u % 3
                    dve.wait_ge(w_dif, u + 1)
                    dve.tensor_tensor(out=w_keep, in0=w_abs[m], in1=w_diff[n], op=ALU.is_gt).then_inc(w_kp, 1)
                    dve.wait_ge(w_kp, u + 1)
                    dve.tensor_tensor(out=w_diff[n], in0=w_abs[m], in1=w_diff[n], op=ALU.add).then_inc(w_step, 1)
                    dve.wait_ge(w_step, 2 * u + 1)
                    dve.tensor_tensor(out=w_diff[n], in0=w_diff[n], in1=w_keep, op=ALU.mult).then_inc(w_step, 1)
                    dve.wait_ge(w_step, 2 * u + 2)
                    need(dve, w_tr, u - 1)
                    dve.tensor_tensor(out=w_tern[n], in0=w_diff[n], in1=w_sign[m], op=ALU.mult).then_inc(w_q, 1)

                for u in range(NTU + 1):
                    if u < NTU:
                        scales(u)
                    if u > 0:
                        quantise(u - 1)

            def largest(m):
                dve.wait_ge(a_in[m], 16)
                dve.tensor_reduce(w_absmax[:, m:m + 1], at_raw[m], AX.XY, ALU.max,
                                  apply_absolute_value=True).then_inc(a_mx, 1)

            def attention_scales():
                dve.wait_ge(a_all, 1)
                dve.tensor_scalar(w_floor[:, :], w_max[:, :], 2.0 ** -40, None, ALU.max).then_inc(sc_step, 1)
                dve.wait_ge(sc_step, 1)
                dve.tensor_scalar(w_pow2[:, :].bitcast(U32), w_floor[:, :].bitcast(U32), 0x7F800000, None,
                                  ALU.bitwise_and).then_inc(sc_step, 1)
                dve.wait_ge(sc_step, 2)
                dve.reciprocal(w_rec[:, :], w_pow2[:, :]).then_inc(sc_step, 1)
                dve.wait_ge(sc_step, 3)
                dve.tensor_scalar(w_scale[:, :], w_rec[:, :], 2.0 ** WS_LOG2, None, ALU.mult).then_inc(sc_step, 1)
                dve.tensor_scalar(exp_scale[:, :], w_pow2[:, Q:Q + 1], w_pow2[:, K:K + 1],
                                  2.0 ** -10 / math.sqrt(DK), ALU.mult, ALU.mult).then_inc(sc_step, 1)
                dve.tensor_scalar(out_scale[:, :], w_pow2[:, V:V + 1], w_pow2[:, O:O + 1],
                                  2.0 ** -(5 + WS_LOG2), ALU.mult, ALU.mult).then_inc(sc_step, 1)
                dve.wait_ge(sc_step, 6)
                dve.tensor_scalar(neg_exp_scale[:, :], exp_scale[:, :], -1.0, None, ALU.mult).then_inc(sc_step, 1)
                dve.memset(kt[:, :, :], 0.0).then_inc(zeroed, 1)
                dve.memset(v_cur[:, :, :, :], 0.0).then_inc(zeroed, 1)
                dve.wait_ge(sc_step, 7)

            def attention_weight(m):
                for half in (0, 1):
                    k = slice(2 * half, 2 * half + 2)
                    dve.wait_ge(a_hi, 2 * m + half + 1)
                    dve.scalar_tensor_tensor(out=wat_lo[m][:, k, :],
                                             in0=ps_w[half][:, :].rearrange("p (k d) -> p k d", k=2),
                                             scalar=w_scale[:, m:m + 1], in1=wat_hi[m][:, k, :], op0=ALU.mult,
                                             op1=ALU.subtract).then_inc(a_lo, 1)

            def flat(ap):
                return ap.rearrange("p a b -> p (a b)")

            def head_view(ap):
                return ap.rearrange("p (h d) -> p h d", d=DK)

            def norm_stats(s, b, ready, n, scale):
                dve.wait_ge(ready, n)
                hold()
                dve.bn_stats(st6[s][:, :], slot(b)).then_inc(d_st[s], 1)
                dve.wait_ge(d_st[s], b + 1)
                hold()
                dve.bn_aggr(mean_var[s][:, :], st6[s][:, :]).then_inc(d_mv[s], 1)
                dve.wait_ge(d_mv[s], b + 1)
                dve.tensor_scalar(var_eps[s][:, :], mean_var[s][:, 1:2], LN_EPS, scale, ALU.add, ALU.mult)\
                   .then_inc(d_ve[s], 1)

            def norm_apply(s, b):
                dve.wait_ge(g_rstd[s], b + 1)
                dve.tensor_scalar(xhat[:, :], slot(b), mean_var[s][:, 0:1], rstd[s][:, 0:1],
                                  ALU.subtract, ALU.mult).then_inc(d_xh[s], 1)

            def rms_stats(s, b):
                dve.wait_ge(a_sq[s], 4 * b + 4)
                dve.tensor_reduce(sq_sum[s][:, :], sq_parts[s][:, :], AX.X, ALU.add).then_inc(d_sqs[s], 1)
                dve.wait_ge(d_sqs[s], b + 1)
                down = 2.0 ** (-2 * HS_LOG2)
                dve.tensor_scalar(sq_mean[s][:, :], sq_sum[s][:, :], down / H, down * RMS_EPS,
                                  ALU.mult, ALU.add).then_inc(d_sqm[s], 1)

            def rms_apply(s, b):
                dve.wait_ge(g_rms[s], b + 1)
                dve.tensor_scalar(h[s][:, :], h[s][:, :], rms_inv[s][:, 0:1], None, ALU.mult).then_inc(d_hn[s], 1)

            def masked_max(b, q):
                dve.wait_ge(p_s, 8 * b + q + 1)
                if q == 0:
                    dve.wait_ge(g_mask, b + 1)
                hold()
                for pair in range(2):
                    for o in range(2):
                        hd = 4 * q + 2 * pair + o
                        at = o * CH + pair * 2 * P
                        r = dve.tensor_tensor_reduce(prob[:, (q // 2) % 2, hd % 8, :], ps_s[:, at:at + 2 * P],
                                                     mask[:, :], 1.0, NEG, ALU.add, ALU.max, row_max[:, hd:hd + 1])
                r.then_inc(d_mx, 1)
                dve.wait_ge(d_mx, 8 * b + q + 1)
                dve.tensor_scalar(exp_bias[:, 4 * q:4 * q + 4], row_max[:, 4 * q:4 * q + 4], neg_exp_scale[:, 0:1],
                                  PROB_LOG2 * math.log(2.0), ALU.mult, ALU.add).then_inc(d_bias, 1)

            def hidden(s, b, c, n):
                dve.wait_ge(a_tanh[s], 4 * b + c + 1)
                dve.scalar_tensor_tensor(out=gate[:, n, :], in0=gate[:, n, :], scalar=1.0, in1=ps_gu[:, 0:CH],
                                         op0=ALU.add, op1=ALU.mult).then_inc(d_gate[s], 1)
                dve.wait_ge(d_gate[s], 4 * b + c + 1)
                dve.wait_ge(p_up[s], 8 * b + 2 * c + 2)
                dve.scalar_tensor_tensor(out=h[s][:, c * CH:(c + 1) * CH], in0=ps_gu[:, CH:2 * CH],
                                         scalar=0.5 * 2.0 ** (-2 * XS_LOG2), in1=gate[:, n, :], op0=ALU.mult,
                                         op1=ALU.mult).then_inc(d_h[s], 1)

            def take_lo(dst, src, hi, ready, n, done):
                dve.wait_ge(ready, n)
                dve.tensor_tensor(out=dst, in0=src, in1=hi, op=ALU.subtract).then_inc(done, 1)

            def normalise_o(b, ct):
                dve.wait_ge(p_pv, 8 * b + 2 * ct + 2)
                o = ps_o[:, 0:8 * 3 * DK].rearrange("p (h t d) -> p h d t", h=8, t=3)
                dve.tensor_reduce(o_sum[:, :, :], o, AX.X, ALU.add).then_inc(d_osum, 1)
                dve.reciprocal(row_inv[:, :], row_sum[:, 8 * ct:8 * ct + 8]).then_inc(d_rinv, 1)
                dve.wait_ge(d_osum, 4 * b + ct + 1)
                dve.wait_ge(d_rinv, 4 * b + ct + 1)
                dve.tensor_tensor(out=head_view(o_norm[:, ct * P:(ct + 1) * P]), in0=o_sum[:, :, :],
                                  in1=row_inv[:, :].unsqueeze(2).to_broadcast([P, 8, DK]),
                                  op=ALU.mult).then_inc(d_on, 1)

            def add_ffn(s, b, done):
                dve.wait_ge(p_dn[s], 4 * b + 4)
                dve.scalar_tensor_tensor(out=slot(b), in0=ps_y[:, :], scalar=0.5 * 2.0 ** -HS_LOG2, in1=slot(b),
                                         op0=ALU.mult, op1=ALU.add).then_inc(done, 1)

            def body(i):
                bL, bA, bQ, bT, bW, bE = i + 1, i, i - 1, i - 2, i - 3, i - 4
                for hs in range(8):
                    up, bu = ("A", bA) if hs < 4 else ("C", bW)
                    dn, bd = ("C", bE) if hs < 4 else ("A", bA)
                    c = hs % 4
                    bp, qp = (bW, 7) if hs < 1 else (bT, hs - 1)
                    bv, qv = (bW, hs + 6) if hs < 2 else (bT, hs - 2)
                    if isinstance(i, int) and i == 0:
                        if hs < 4:
                            largest(hs)
                        elif hs == 4:
                            attention_scales()
                        else:
                            attention_weight(hs - 5)
                    if hs == 0 and on(bQ):
                        norm_stats("B", bQ, d_x1, bQ + 1, 2.0 ** (-2 * XS_LOG2))
                    if hs == 1 and on(bQ):
                        dve.wait_ge(a_q, bQ + 1)
                        dve.scalar_tensor_tensor(out=qk4[:, :, 1, :], in0=head_view(ps_m[:, :]),
                                                 scalar=2.0 ** -DOWN_LOG2, in1=qk4[:, :, 0, :], op0=ALU.mult,
                                                 op1=ALU.subtract).then_inc(d_qlo, 1)
                        dve.wait_ge(d_qlo, bQ + 1)
                        dve.tensor_copy(qk4[:, :, 2:4, :], qk4[:, :, 0:2, :]).then_inc(d_q, 1)
                    if hs == 2 and on(bQ):
                        dve.wait_ge(p_qt, 2 * bQ + 2)
                        dve.tensor_copy(qt_next[:, 8:16, :], ps_m16).then_inc(d_qt, 1)
                    if hs == 2 and on(bT):
                        dve.wait_ge(g_v, bT + 1)
                        need(dve, p_pv, 8 * bT)
                        dve.tensor_copy(v_prev[:, :, :, :], v_cur[:, :, :, :]).then_inc(d_vold, 1)
                        dve.wait_ge(d_vold, bT + 1)
                        dve.tensor_copy(v_cur[:, :, :, :], v_next[:, :, :, :]).then_inc(d_vshift, 1)
                    if hs == 3 and on(bW):
                        dve.wait_ge(p_wo, bW + 1)
                        dve.scalar_tensor_tensor(out=slot(bW), in0=ps_m[:, :], scalar=out_scale[:, 0:1],
                                                 in1=slot(bW), op0=ALU.mult, op1=ALU.add).then_inc(d_x2, 1)
                        norm_stats("C", bW, d_x2, bW + 1, 2.0 ** (-2 * XS_LOG2))
                    if hs == 4 and on(bQ):
                        k4 = qk4[:, :, :, :].rearrange("p h (a b) d -> p h a b d", b=2)
                        dve.wait_ge(a_k, bQ + 1)
                        dve.scalar_tensor_tensor(out=qk4[:, :, 2, :], in0=head_view(ps_m[:, :]),
                                                 scalar=2.0 ** -DOWN_LOG2, in1=qk4[:, :, 0, :], op0=ALU.mult,
                                                 op1=ALU.subtract).then_inc(d_klo, 1)
                        dve.wait_ge(d_klo, bQ + 1)
                        dve.tensor_copy(k4[:, :, :, 1, :], k4[:, :, :, 0, :]).then_inc(d_k, 1)
                    if on(bT):
                        masked_max(bT, hs)
                    if hs == 0 and on(bQ):
                        need(dve, p_xt["A"], last(i) + 1)
                        need(dve, g_v, bQ)
                        norm_apply("B", bQ)
                    if hs == 3 and on(bW):
                        if on(bQ):
                            dve.wait_ge(p_xt["B"], bQ + 1)
                        else:
                            dve.wait_ge(g_v, NB)
                            dve.wait_ge(p_xt["C"], bW)
                        norm_apply("C", bW)
                    if hs == 6 and on(bL):
                        if on(bW):
                            dve.wait_ge(p_xt["C"], bW + 1)
                        elif on(bQ):
                            dve.wait_ge(p_xt["B"], bQ + 1)
                        else:
                            need(dve, p_xt["A"], bL)
                        norm_apply("A", bL)
                    if hs == 7 and on(bQ):
                        if on(bT):
                            dve.wait_ge(p_s, 8 * bT + 8)
                        dve.wait_ge(d_qt, 2 * bQ + 2)
                        dve.wait_ge(a_kt, 2 * bQ + 2)
                        dve.tensor_copy(kt[:, :, 0:P], kt[:, :, P:2 * P]).then_inc(d_kold, 1)
                        dve.tensor_copy(qt[:, :, :], qt_next[:, :, :])
                        dve.wait_ge(d_kold, bQ + 1)
                        dve.tensor_copy(kt[:, :, P:2 * P], kt_next[:, :, :]).then_inc(d_kshift, 1)
                    if on(bu):
                        hidden(up, bu, c, hs % 2)
                    if on(bd):
                        take_lo(flat(ht_lo[:, c % 2, :, :]), ps_ht[:, :], flat(ht_hi[:, c % 2, :, :]),
                                a_ht[dn], 4 * bd + c + 1, d_ht[dn])
                    if hs == 1 and on(bQ):
                        dve.wait_ge(p_qt, 2 * bQ + 1)
                        dve.tensor_copy(qt_next[:, 0:8, :], ps_m16).then_inc(d_qt, 1)
                    if hs == 0 and on(bQ):
                        take_lo(flat(xt_lo["B"][:, :, :]), ps_m[:, :], flat(xt_hi["B"][:, :, :]),
                                a_xt["B"], bQ + 1, d_xt["B"])
                    if hs == 2 and on(bW):
                        take_lo(flat(ot_lo[:, :, :]), ps_m[:, :], flat(ot_hi[:, :, :]), a_ot, bW + 1, d_ot)
                    if hs == 3 and on(bW):
                        take_lo(flat(xt_lo["C"][:, :, :]), ps_m[:, :], flat(xt_hi["C"][:, :, :]),
                                a_xt["C"], bW + 1, d_xt["C"])
                    if on(bp):
                        take_lo(flat(pt_lo[:, :, :]), ps_s[:, :], flat(pt_hi[:, :, :]), a_pt, 8 * bp + qp + 1, d_pt)
                    if hs == 6 and on(bL):
                        take_lo(flat(xt_lo["A"][:, :, :]), ps_m[:, :], flat(xt_hi["A"][:, :, :]),
                                a_xt["A"], bL + 1, d_xt["A"])
                    if hs == 3 and on(bA):
                        rms_stats("A", bA)
                    if hs == 7 and on(bW):
                        rms_stats("C", bW)
                    if hs % 2 and on(bv):
                        normalise_o(bv, qv // 2)
                    if hs == 3 and on(bA):
                        rms_apply("A", bA)
                    if hs == 7 and on(bW):
                        rms_apply("C", bW)
                    if hs == 3 and on(bE):
                        add_ffn("C", bE, d_x3)
                    if hs == 5 and on(bL):
                        norm_stats("A", bL, x_in, 16 * (bL + 1), 2.0 ** (-2 * XS_LOG2))
                    if hs == 7 and on(bQ):
                        if on(bL):
                            dve.wait_ge(p_xt["A"], bL + 1)
                        elif on(bW):
                            dve.wait_ge(p_xt["C"], bW + 1)
                        dve.wait_ge(a_v, bQ + 1)
                        dve.scalar_tensor_tensor(out=head_view(xhat[:, :]), in0=head_view(ps_m[:, :]),
                                                 scalar=2.0 ** -DOWN_LOG2, in1=v_next[:, :, 0, :], op0=ALU.mult,
                                                 op1=ALU.subtract).then_inc(d_v, 1)
                    if hs == 7 and on(bA):
                        add_ffn("A", bA, d_x1)
                if isinstance(i, int) and i == 0:
                    attention_weight(3)

            all_iterations(dve, body, ternary_weights)

        @block.tensor
        def _(pe):
            pe.wait_ge(ids, 2)

            def ternary_weights():
                for u in range(NTU):
                    pe.wait_ge(w_q, u + 1)
                    need(pe, w_st, u - 1)
                    bank = ps_w[u % 2][:, :].bitcast(BF16)
                    for a in range(4):
                        for k in range(4):
                            if u < NGU:
                                src, dst = a * 512 + k * P, k * 512 + a * P
                            else:
                                src = dst = (4 * a + k) * P
                            t = pe.transpose(bank[:, dst:dst + P], w_tern[u % 2][:, src:src + P], idb[:, :])
                    t.then_inc(w_tr, 1)

            def attention_weight(m):
                pe.wait_ge(a_in[m], 16)
                need(pe, a_hi, 2 * m)
                need(pe, a_lo, 2 * m)
                for k in range(4):
                    for a in range(4):
                        at = (k % 2) * 512 + a * P
                        t = pe.transpose(ps_w[k // 2][:, at:at + P], at_raw[m][:, a, k * P:(k + 1) * P], id32[:, :])
                t.then_inc(a_tr, 1)

            def xt_piece(s, b):
                pe.wait_ge(d_xh[s], b + 1)
                for k in range(KD):
                    t = pe.transpose(ps_m[:, k * P:(k + 1) * P], xhat[:, k * P:(k + 1) * P], id32[:, :])
                t.then_inc(p_xt[s], 1)

            def up(s, b, c):
                for half in (0, 1):
                    n = 0
                    for k in range(KD):
                        for part in (xt_hi[s], xt_lo[s]):
                            t = pe.matmul(ps_gu[:, half * CH:(half + 1) * CH], part[:, k, :],
                                          wgu_t[:, k, half * H + c * CH:half * H + (c + 1) * CH],
                                          start=(n == 0), stop=(n == 2 * KD - 1))
                            n += 1
                    t.then_inc(p_up[s], 1)

            def hidden_t(s, b, g):
                for j in range(4):
                    at = (4 * g + j) * P
                    t = pe.transpose(ps_ht[:, j * P:(j + 1) * P], h[s][:, at:at + P], id32[:, :])
                t.then_inc(p_ht[s], 1)

            def down(s, b, g):
                pe.wait_ge(d_ht[s], 4 * b + g + 1)
                for j in range(4):
                    for part in (ht_hi, ht_lo):
                        t = pe.matmul(ps_y[:, :], part[:, g % 2, j, :], wp_t[:, 4 * g + j, :],
                                      start=(g == 0 and j == 0 and part is ht_hi),
                                      stop=(g == 3 and j == 3 and part is ht_lo))
                t.then_inc(p_dn[s], 1)

            def project(m, hi, lo, done):
                n = 0
                for k in range(KD):
                    for part, w in ((hi, wat_hi), (hi, wat_lo), (lo, wat_hi)):
                        t = pe.matmul(ps_m[:, :], part[:, k, :], w[m][:, k, :], start=(n == 0), stop=(n == 3 * KD - 1))
                        n += 1
                t.then_inc(done, 1)

            def heads_t(f, done):
                for j in range(8):
                    pair = 8 * f + j
                    t = pe.transpose(ps_m16[:, j, :],
                                     qk4[:, 2 * pair:2 * pair + 2, :, :].rearrange("p a b c -> p (a b c)"), id16[:, :])
                t.then_inc(done, 1)

            def scores(b, q):
                for pair in range(2):
                    for o in range(2):
                        at = o * CH + pair * 2 * P
                        rows = slice(64 * o, 64 * o + 64)
                        t = pe.matmul(ps_s[:, at:at + 2 * P], qt[rows, 2 * q + pair, :], kt[rows, 2 * q + pair, :],
                                      start=True, stop=True)
                t.then_inc(p_s, 1)

            def prob_t(b, q):
                pe.wait_ge(a_exp, 8 * b + q + 1)
                for j in range(4):
                    for half in range(2):
                        at = (2 * j + half) * P
                        t = pe.transpose(ps_s[:, at:at + P],
                                         prob[:, (q // 2) % 2, (4 * q + j) % 8, half * P:(half + 1) * P], id32[:, :])
                t.then_inc(p_pt, 1)

            def prob_v(b, q):
                pe.wait_ge(d_pt, 8 * b + q + 1)
                for j in range(4):
                    hd = 4 * q + j
                    at = (hd % 8) * 3 * DK
                    n = 0
                    for half, v in enumerate((v_prev, v_cur)):
                        for part in (pt_hi, pt_lo):
                            t = pe.matmul(ps_o[:, at:at + 3 * DK], part[:, 2 * j + half, :],
                                          v[:, hd, :, :].rearrange("p a b -> p (a b)"), start=(n == 0), stop=(n == 3))
                            n += 1
                t.then_inc(p_pv, 1)

            def body(i):
                bL, bA, bQ, bT, bW, bE = i + 1, i, i - 1, i - 2, i - 3, i - 4
                for hs in range(8):
                    c = hs % 4
                    bp, qp = (bW, 7) if hs < 1 else (bT, hs - 1)
                    bv, qv = (bW, hs + 6) if hs < 2 else (bT, hs - 2)
                    if isinstance(i, int) and i == 0 and hs >= 4:
                        if hs == 4:
                            pe.wait_ge(d_h["A"], 4)
                        attention_weight(hs - 4)
                    if hs == 1 and on(bQ):
                        pe.wait_ge(d_xt["B"], bQ + 1)
                        project(Q, xt_hi["B"], xt_lo["B"], p_q)
                    if hs == 2 and on(bQ):
                        pe.wait_ge(d_qt, 2 * bQ + 1)
                        heads_t(1, p_qt)
                    if hs == 3 and on(bW):
                        pe.wait_ge(d_ot, bW + 1)
                        project(O, ot_hi, ot_lo, p_wo)
                    if hs == 4 and on(bQ):
                        if on(bW):
                            pe.wait_ge(d_xt["C"], bW + 1)
                        else:
                            pe.wait_ge(d_qt, 2 * bQ + 2)
                        project(K, xt_hi["B"], xt_lo["B"], p_k)
                    if hs == 5 and on(bQ):
                        pe.wait_ge(a_kt, 2 * bQ + 1)
                        heads_t(1, p_kt)
                    if on(bT):
                        if hs == 0:
                            pe.wait_ge(d_kshift, bT + 1)
                        need(pe, d_pt, 8 * bT + hs - 1)
                        scores(bT, hs)
                    if hs < 4 and on(bA):
                        if hs == 0:
                            pe.wait_ge(d_xt["A"], bA + 1)
                            need(pe, d_h["C"], 4 * (i - 4) + 4)
                            if isinstance(i, int) and i - 4 < 0:
                                need(pe, d_h["A"], 4 * bA)
                        else:
                            pe.wait_ge(d_h["A"], 4 * bA + c)
                        up("A", bA, c)
                    if hs >= 4 and on(bW):
                        if hs == 4:
                            pe.wait_ge(d_xt["C"], bW + 1)
                            pe.wait_ge(d_h["A"], 4 * last(i) + 4)
                            need(pe, d_h["C"], 4 * bW)
                        else:
                            pe.wait_ge(d_h["C"], 4 * bW + c)
                        up("C", bW, c)
                    if hs < 4 and on(bE):
                        if hs == 0:
                            pe.wait_ge(d_hn["C"], bE + 1)
                            pe.wait_ge(d_ht["A"], 4 * last(i - 1) + 4)
                            need(pe, d_ht["C"], 4 * bE)
                        else:
                            pe.wait_ge(d_ht["C"], 4 * bE + c)
                        hidden_t("C", bE, c)
                    if hs >= 4 and on(bA):
                        if hs == 4:
                            pe.wait_ge(d_hn["A"], bA + 1)
                            need(pe, d_ht["C"], 4 * (i - 4) + 4)
                            need(pe, d_ht["A"], 4 * bA)
                        else:
                            pe.wait_ge(d_ht["A"], 4 * bA + c)
                        hidden_t("A", bA, c)
                    if on(bv):
                        if qv == 0:
                            pe.wait_ge(d_vshift, bv + 1)
                        if qv % 2 == 0:
                            need(pe, d_on, 4 * bv + qv // 2)
                        prob_v(bv, qv)
                    if on(bp):
                        if on(bT):
                            pe.wait_ge(d_bias, 8 * bT + hs + 1)
                        else:
                            need(pe, d_pt, 8 * bp + qp)
                        prob_t(bp, qp)
                    if hs == 0 and on(bQ):
                        pe.wait_ge(d_xt["A"], last(i) + 1)
                        need(pe, d_v, bQ)
                        xt_piece("B", bQ)
                    if hs == 1 and on(bQ):
                        pe.wait_ge(d_q, bQ + 1)
                        heads_t(0, p_qt)
                    if hs == 2 and on(bW):
                        if on(bQ):
                            pe.wait_ge(d_qt, 2 * bQ + 2)
                        else:
                            pe.wait_ge(d_v, NB)
                            pe.wait_ge(d_xt["C"], bW)
                        pe.wait_ge(d_on, 4 * bW + 4)
                        for k in range(KD):
                            t = pe.transpose(ps_m[:, k * P:(k + 1) * P], o_norm[:, k * P:(k + 1) * P], id32[:, :])
                        t.then_inc(p_ot, 1)
                    if hs == 3 and on(bW):
                        xt_piece("C", bW)
                    if hs == 4 and on(bQ):
                        pe.wait_ge(d_k, bQ + 1)
                        heads_t(0, p_kt)
                    if hs == 6 and on(bL):
                        if on(bQ):
                            pe.wait_ge(a_kt, 2 * bQ + 2)
                        else:
                            need(pe, d_xt["A"], bL)
                        xt_piece("A", bL)
                    if hs == 7 and on(bQ):
                        if on(bL):
                            pe.wait_ge(d_xt["A"], bL + 1)
                        else:
                            pe.wait_ge(a_kt, 2 * bQ + 2)
                        project(V, xt_hi["B"], xt_lo["B"], p_v)
                    if hs < 4 and on(bE):
                        if hs == 0:
                            pe.wait_ge(d_x1, last(i - 1) + 1)
                            need(pe, d_x3, bE)
                        down("C", bE, c)
                    if hs >= 4 and on(bA):
                        if hs == 4:
                            need(pe, d_x3, i - 3)
                            need(pe, d_x1, bA)
                        down("A", bA, c)

            all_iterations(pe, body, ternary_weights)
_INS=['L0_attn_x','L0_attn_Wq','L0_attn_Wk','L0_attn_Wv','L0_attn_Wo','L0_ffn_w_gate_up','L0_ffn_w_proj']
def kernel(**inputs):
    import numpy as _np
    import concourse.bacc as _bacc
    from concourse import mybir as _mybir
    from concourse.bass_utils import run_bass_kernel_spmd as _run
    nc=_bacc.Bacc("TRN2",target_bir_lowering=False,num_devices=1)
    arrays,args={},[]
    for name in _INS:
        a=_np.ascontiguousarray(inputs[name])
        arrays[f"in_{name}_dram"]=a
        args.append(nc.dram_tensor(f"in_{name}_dram",a.shape,_mybir.dt.from_np(a.dtype),kind="ExternalInput").ap())
    args.append(nc.dram_tensor("out_0_dram",(8,512,512),_mybir.dt.float32,kind="ExternalOutput").ap())
    macaron(nc,*args)
    r=_run(nc,[arrays],core_ids=[0])
    return r.results[0]["out_0_dram"]
```

```python
from contextlib import ExitStack
import math

import concourse.bass as bass
from concourse import mybir

F32 = mybir.dt.float32
F16 = mybir.dt.float16
BF16 = mybir.dt.bfloat16
U32 = mybir.dt.uint32
ALU = mybir.AluOpType
ACT = mybir.ActivationFunctionType
AX = mybir.AxisListType
RMAX = bass.bass_isa.ReduceOp.max

P = 128
HEADS = 32
LN_EPS = 1e-5
RMS_EPS = 2.0 ** -23
CLIP_MIN = 1.0011717677116394e-08
NEG = -3.0e38
PROB_LOG2 = 15


def macaron(nc, x, Wq, Wk, Wv, Wo, w_gate_up, w_proj, out):
    B, S, D = x.shape
    H = w_proj.shape[1]
    KD, KH = D // P, H // P
    DK = D // HEADS
    NB = B * S // P
    BPS = S // P
    CH = 512
    NC = H // CH
    XS_LOG2 = 11
    WS_LOG2 = 13
    DOWN_LOG2 = XS_LOG2 + WS_LOG2 - 5
    HS_LOG2 = 10
    RING = 7
    assert D == 512 and H == 2048 and DK == 16 and NC == 4

    xf = x.rearrange("b t d -> (b t) d")
    of = out.rearrange("b t d -> (b t) d")
    gu_units = w_gate_up.rearrange("(u t p) d -> u p t d", t=4, p=P)
    wp_units = w_proj.rearrange("(u p) h -> u p h", p=P)
    at_units = [w.rearrange("(t p) d -> p t d", p=P) for w in (Wq, Wk, Wv, Wo)]
    NGU, NWP = 2 * H // 512, D // P
    NTU = NGU + NWP
    G64 = 32

    with ExitStack() as ctx:
        def sb(name, shape, dt):
            return ctx.enter_context(nc.sbuf_tensor(name, shape, dt))

        def psum(name, shape):
            return ctx.enter_context(nc.psum_tensor(name, shape, F32))

        def sem(name):
            return ctx.enter_context(nc.semaphore(name))

        ps_s = psum("ps_s", [P, 1024])
        ps_gu = psum("ps_gu", [P, 1024])
        ps_y = psum("ps_y", [P, CH])
        ps_ht = psum("ps_ht", [P, CH])
        ps_o = psum("ps_o", [P, CH])
        ps_m = psum("ps_m", [P, CH])
        ps_m16 = ps_m[:, :].bitcast(F16).rearrange("p (a b) -> p a b", b=P)

        wgu_t = sb("wgu_t", [P, KD, 2 * H], BF16)
        wp_t = sb("wp_t", [P, KH, D], BF16)
        wat_hi = [sb(f"w{n}_hi", [P, KD, D], F16) for n in "qkvo"]
        wat_lo = [sb(f"w{n}_lo", [P, KD, D], F16) for n in "qkvo"]
        Q, K, V, O = range(4)
        stream = sb("stream", [P, RING, D], F32)
        xhat = sb("xhat", [P, D], F32)
        v_rest = sb("v_rest", [P, D], F32)
        xt_hi = {s: sb(f"xt_hi_{s}", [P, KD, P], F16) for s in "ABC"}
        xt_lo = {s: sb(f"xt_lo_{s}", [P, KD, P], F16) for s in "ABC"}
        gate = sb("gate", [P, 2, CH], F32)
        h = {s: sb(f"h_{s}", [P, H], F32) for s in "AC"}
        ht_hi = sb("ht_hi", [P, 2, 4, P], F16)
        ht_lo = sb("ht_lo", [P, 2, 4, P], F16)
        qk4 = sb("qk4", [P, HEADS, 4, DK], F16)
        qt = sb("qt", [P, 2, HEADS // 2, P], F16)
        kt = sb("kt", [P, HEADS // 2, BPS, P], F16)
        v = sb("v", [P, BPS, HEADS, 3, DK], BF16)
        prob = sb("prob", [P, 2, 4, 2 * P], F32)
        pt_hi = sb("pt_hi", [P, 8, P], F16)
        pt_lo = sb("pt_lo", [P, 8, P], F16)
        o_sum = sb("o_sum", [P, 8, DK], F32)
        o_norm = sb("o_norm", [P, D], F32)
        ot_hi = sb("ot_hi", [P, KD, P], F16)
        ot_lo = sb("ot_lo", [P, KD, P], F16)
        id32 = sb("id32", [P, P], F32)
        id16 = sb("id16", [P, P], F16)
        idb = sb("idb", [P, P], BF16)
        mask = sb("mask", [P, 2 * P], F32)
        zeros = sb("zeros", [P, P], F32)
        neg_half = sb("neg_half", [P, 1], F32)
        carrier = sb("carrier", [1, 384], F32)
        row_max = sb("row_max", [P, HEADS], F32)
        exp_bias = sb("exp_bias", [P, HEADS], F32)
        row_sum = sb("row_sum", [P, HEADS], F32)
        row_inv = sb("row_inv", [P, 8], F32)
        st6 = {s: sb(f"st6_{s}", [P, 6], F32) for s in "ABC"}
        mean_var = {s: sb(f"mean_var_{s}", [P, 2], F32) for s in "ABC"}
        var_eps = {s: sb(f"var_eps_{s}", [P, 1], F32) for s in "ABC"}
        rstd = {s: sb(f"rstd_{s}", [P, 1], F32) for s in "ABC"}
        sq_parts = {s: sb(f"sq_parts_{s}", [P, NC], F32) for s in "AC"}
        sq_sum = {s: sb(f"sq_sum_{s}", [P, 1], F32) for s in "AC"}
        sq_mean = {s: sb(f"sq_mean_{s}", [P, 1], F32) for s in "AC"}
        rms_inv = {s: sb(f"rms_inv_{s}", [P, 1], F32) for s in "AC"}
        w_absmax = sb("w_absmax", [P, 4], F32)
        w_max = sb("w_max", [P, 4], F32)
        w_floor = sb("w_floor", [P, 4], F32)
        w_pow2 = sb("w_pow2", [P, 4], F32)
        w_rec = sb("w_rec", [P, 4], F32)
        w_scale = sb("w_scale", [P, 4], F32)
        out_scale = sb("out_scale", [P, 1], F32)
        exp_scale = sb("exp_scale", [P, 1], F32)
        neg_exp_scale = sb("neg_exp_scale", [P, 1], F32)
        grp_sum = sb("grp_sum", [P, 2, G64], F32)
        grp_scale = sb("grp_scale", [P, 2, G64], BF16)
        kt_4k = [kt[:, 4 * n:4 * n + 4, :, :].rearrange("p a b c -> p (a b c)").bitcast(BF16) for n in range(4)]
        qt_4k = [qt[:, n, :, :].rearrange("p a b -> p (a b)").bitcast(BF16) for n in range(2)]
        prob_4k = [prob[:, n, :, :].rearrange("p a b -> p (a b)").bitcast(BF16) for n in range(2)]
        w_raw = [h["A"], h["C"]]
        w_abs = kt_4k[0:3]
        w_sign = [kt_4k[3], gate[:, :, :].rearrange("p a b -> p (a b)").bitcast(BF16), qt_4k[0]]
        w_diff = [qk4[:, :, :, :].rearrange("p a b c -> p (a b c)").bitcast(BF16), qt_4k[1]]
        w_keep = v[:, :, :, :, :].rearrange("p a b c d -> p (a b c d)")[:, 0:2048]
        w_tern = prob_4k
        at_raw = [stream[:, 2:6, :], h["C"][:, :].rearrange("p (t d) -> p t d", t=4),
                  kt[:, 0:8, :, :].rearrange("p (t a) b c -> p t (a b c)", t=4).bitcast(F32),
                  prob[:, :, :, :].rearrange("p a (t b) c -> p (a t) (b c)", t=2)]
        ps_w = [ps_s, ps_gu]

        consts = sem("consts")
        ids = sem("ids")
        w_in = [sem(f"w_in{n}") for n in (0, 1)]
        w_parts = sem("w_parts")
        w_sum = sem("w_sum")
        w_grp = sem("w_grp")
        w_dif = sem("w_dif")
        w_kp = sem("w_kp")
        w_step = sem("w_step")
        w_q = sem("w_q")
        w_tr = sem("w_tr")
        w_st = sem("w_st")
        a_in = [sem(f"a_in{m}") for m in range(4)]
        a_mx = sem("a_mx")
        a_all = sem("a_all")
        sc_step = sem("sc_step")
        a_tr = sem("a_tr")
        a_hi = sem("a_hi")
        a_lo = sem("a_lo")
        p_xt = {s: sem(f"p_xt_{s}") for s in "ABC"}
        p_up = {s: sem(f"p_up_{s}") for s in "AC"}
        p_ht = {s: sem(f"p_ht_{s}") for s in "AC"}
        p_dn = {s: sem(f"p_dn_{s}") for s in "AC"}
        p_q, p_k, p_v = sem("p_q"), sem("p_k"), sem("p_v")
        p_qt, p_kt = sem("p_qt"), sem("p_kt")
        p_s = sem("p_s")
        p_pt = sem("p_pt")
        p_pv = sem("p_pv")
        p_ot, p_wo = sem("p_ot"), sem("p_wo")
        a_xt = {s: sem(f"a_xt_{s}") for s in "ABC"}
        a_tanh = {s: sem(f"a_tanh_{s}") for s in "AC"}
        a_sq = {s: sem(f"a_sq_{s}") for s in "AC"}
        a_ht = {s: sem(f"a_ht_{s}") for s in "AC"}
        a_q, a_k, a_v = sem("a_q"), sem("a_k"), sem("a_v")
        a_kt = sem("a_kt")
        a_exp = sem("a_exp")
        a_pt = sem("a_pt")
        a_ot = sem("a_ot")
        d_xt = {s: sem(f"d_xt_{s}") for s in "ABC"}
        d_gate = {s: sem(f"d_gate_{s}") for s in "AC"}
        d_h = {s: sem(f"d_h_{s}") for s in "AC"}
        d_sqs = {s: sem(f"d_sqs_{s}") for s in "AC"}
        d_sqm = {s: sem(f"d_sqm_{s}") for s in "AC"}
        d_hn = {s: sem(f"d_hn_{s}") for s in "AC"}
        d_ht = {s: sem(f"d_ht_{s}") for s in "AC"}
        d_qlo, d_klo = sem("d_qlo"), sem("d_klo")
        d_q, d_k, d_v = sem("d_q"), sem("d_k"), sem("d_v")
        d_qt = sem("d_qt")
        d_mx = sem("d_mx")
        d_bias = sem("d_bias")
        d_pt = sem("d_pt")
        d_ot = sem("d_ot")
        d_osum, d_rinv = sem("d_osum"), sem("d_rinv")
        d_on = sem("d_on")
        d_x1, d_x2, d_x3 = sem("d_x1"), sem("d_x2"), sem("d_x3")
        d_st = {s: sem(f"d_st_{s}") for s in "ABC"}
        d_mv = {s: sem(f"d_mv_{s}") for s in "ABC"}
        d_ve = {s: sem(f"d_ve_{s}") for s in "ABC"}
        d_xh = {s: sem(f"d_xh_{s}") for s in "ABC"}
        g_rstd = {s: sem(f"g_rstd_{s}") for s in "ABC"}
        g_rms = {s: sem(f"g_rms_{s}") for s in "AC"}
        g_vm, g_v = sem("g_vm"), sem("g_v")
        x_in = [sem(f"x_in{n}") for n in (0, 1)]
        x_out = sem("x_out")

        NCONST = 7

        def need(eng, s, n):
            if not isinstance(n, int) or n > 0:
                eng.wait_ge(s, n)

        def last(b):
            return min(b, NB - 1) if isinstance(b, int) else b

        places = iter(range(384))

        def place_of_carrier():
            n = next(places)
            return carrier[0:1, n:n + 1]

        def on(b):
            return not isinstance(b, int) or 0 <= b < NB

        def slot(b):
            if isinstance(b, int):
                return stream[:, b % RING, :]
            return stream[:, bass.ds((b + RING) % RING, 1), :].rearrange("p a d -> p (a d)")

        STEADY, END = 5, NB + 4
        STEADY_END = STEADY + (NB - 1 - STEADY) // BPS * BPS

        def ternary_done(eng):
            eng.wait_ge(w_st, NTU)

        def attention_weights_done(eng):
            eng.wait_ge(a_hi, 8)
            eng.wait_ge(a_lo, 8)
            eng.wait_ge(sc_step, 7)

        def all_iterations(eng, body, ternary_weights):
            body(-1, BPS - 1)
            ternary_weights()
            ternary_done(eng)
            body(0, 0)
            attention_weights_done(eng)
            for i in range(1, STEADY):
                body(i, i % BPS)
            with eng.Fori(0, (STEADY_END - STEADY) // BPS) as j:
                for n in range(BPS):
                    body(BPS * j + (STEADY + n), (STEADY + n) % BPS)
            for i in range(STEADY_END, END):
                body(i, i % BPS)

        def prob_t_view(tiles, place):
            if place:
                return tiles.rearrange("p a b -> p (a b)")
            return tiles.rearrange("p (j h) b -> p j h b", h=2)[:, :, 1, :]

        def spare(i, hs):
            if not isinstance(i, int):
                return None
            up_missing, down_missing = (not on(i), not on(i - 4)) if hs < 4 else (not on(i - 3), not on(i))
            return "gu" if up_missing else "ht_y" if down_missing else None

        def pt_banks(i, hs):
            return {None: (ps_s[:, 0:CH], ps_s[:, CH:2 * CH]), "gu": (ps_gu[:, 0:CH], ps_gu[:, CH:2 * CH]),
                    "ht_y": (ps_ht[:, :], ps_y[:, :])}[spare(i, hs)]

        def ps_t_view(bank, place):
            return bank if place else bank.rearrange("p (j h b) -> p j h b", h=2, b=P)[:, :, 1, :]

        block = ctx.enter_context(nc.Block())

        @block.sync
        def _(sp):
            def ternary_weights():
                for u in range(NTU):
                    need(sp, w_parts, u - 1)
                    if u < NGU:
                        sp.dma_start(w_raw[u % 2][:, :].rearrange("p (t d) -> p t d", t=4),
                                     gu_units[u]).then_inc(w_in[u % 2], 16)
                    else:
                        sp.dma_start(w_raw[u % 2][:, :], wp_units[u - NGU]).then_inc(w_in[u % 2], 16)
                sp.dma_start(at_raw[Q], at_units[Q]).then_inc(a_in[Q], 16)
                sp.wait_ge(w_parts, NTU)
                sp.dma_start(at_raw[K], at_units[K]).then_inc(a_in[K], 16)
                sp.wait_ge(w_q, NTU)
                sp.dma_start(at_raw[V], at_units[V]).then_inc(a_in[V], 16)
                sp.wait_ge(w_tr, NTU)
                sp.dma_start(at_raw[O], at_units[O]).then_inc(a_in[O], 16)

            def body(i, place):
                b = i + 1
                if on(b):
                    need(sp, x_out, 16 * (b - 5))
                    if isinstance(b, int):
                        need(sp, x_in[b % 2], 16 * (b // 2))
                    rows = slice(b * P, (b + 1) * P) if isinstance(b, int) else bass.ds(b * P, P)
                    sp.dma_start(slot(b), xf[rows, :]).then_inc(x_in[(place + 1) % 2], 16)
                b = i - 4
                if on(b):
                    sp.wait_ge(d_x3, b + 1)
                    rows = slice(b * P, (b + 1) * P) if isinstance(b, int) else bass.ds(b * P, P)
                    sp.dma_start(of[rows, :], slot(b)).then_inc(x_out, 16)

            all_iterations(sp, body, ternary_weights)
            sp.wait_ge(x_out, 16 * NB)

        @block.gpsimd
        def _(pool):
            pool.memset(id32[:, :], 0.0).then_inc(consts, 1)
            pool.memset(mask[:, :], 0.0).then_inc(consts, 1)
            pool.memset(zeros[:, :], 0.0).then_inc(consts, 1)
            pool.memset(neg_half[:, :], -0.5).then_inc(consts, 1)
            pool.wait_ge(consts, 4)
            pool.affine_select(out=id32[:, :], in_=id32[:, :], compare_op=ALU.not_equal, fill=1.0, base=0,
                               pattern=[[-1, P]], channel_multiplier=1).then_inc(consts, 1)
            pool.affine_select(out=mask[:, 0:P], in_=mask[:, 0:P], compare_op=ALU.is_ge, fill=NEG, base=0,
                               pattern=[[1, P]], channel_multiplier=-1).then_inc(consts, 1)
            pool.affine_select(out=mask[:, P:2 * P], in_=mask[:, P:2 * P], compare_op=ALU.is_ge, fill=NEG, base=0,
                               pattern=[[-1, P]], channel_multiplier=1).then_inc(consts, 1)

            def ternary_weights():
                for u in range(NTU):
                    pool.wait_ge(w_grp, u + 1)
                    need(pool, w_q, u - 1)
                    pool.tensor_tensor(out=w_diff[u % 2].rearrange("p (g k) -> p g k", g=G64),
                                       in0=grp_scale[:, u % 2, :].unsqueeze(2).to_broadcast([P, G64, 64]),
                                       in1=w_abs[u % 3].rearrange("p (g k) -> p g k", g=G64),
                                       op=ALU.subtract).then_inc(w_dif, 1)

            pool.wait_ge(consts, NCONST)

            def power(s, dst, src, ready, done, b):
                pool.wait_ge(ready, b + 1)
                pool.tensor_tensor(out=dst[:, :], in0=src[:, :], in1=neg_half[:, :], op=ALU.pow).then_inc(done, 1)

            def body(i, place):
                if isinstance(i, int) and i == 0:
                    pool.wait_ge(a_mx, 4)
                    pool.partition_all_reduce(w_max[:, :], w_absmax[:, :], P, RMAX).then_inc(a_all, 1)
                if on(i - 1):
                    power("B", rstd["B"], var_eps["B"], d_ve["B"], g_rstd["B"], i - 1)
                if on(i - 3):
                    power("C", rstd["C"], var_eps["C"], d_ve["C"], g_rstd["C"], i - 3)
                if on(i):
                    power("A", rms_inv["A"], sq_mean["A"], d_sqm["A"], g_rms["A"], i)
                if on(i + 1):
                    power("A", rstd["A"], var_eps["A"], d_ve["A"], g_rstd["A"], i + 1)
                if on(i - 3):
                    power("C", rms_inv["C"], sq_mean["C"], d_sqm["C"], g_rms["C"], i - 3)
                if on(i - 1):
                    b = i - 1
                    pool.wait_ge(d_v, b + 1)
                    vr = v_rest[:, :].rearrange("p (h d) -> p h d", d=DK)
                    mine = v[:, (place - 1) % BPS, :, :, :]
                    pool.tensor_tensor(out=mine[:, :, 1, :], in0=vr,
                                       in1=zeros[:, 0:1].unsqueeze(2).to_broadcast([P, HEADS, DK]),
                                       op=ALU.add).then_inc(g_vm, 1)
                    pool.wait_ge(g_vm, b + 1)
                    pool.tensor_tensor(out=mine[:, :, 2, :], in0=vr, in1=mine[:, :, 1, :],
                                       op=ALU.subtract).then_inc(g_v, 1)

            all_iterations(pool, body, ternary_weights)

        @block.scalar
        def _(act):
            def ternary_weights():
                def parts(u):
                    act.wait_ge(w_in[u % 2], 16 * (u // 2 + 1))
                    need(act, w_q, u - 2)
                    act.activation(w_abs[u % 3], w_raw[u % 2][:, :], ACT.Abs)
                    act.activation(w_sign[u % 3], w_raw[u % 2][:, :], ACT.Sign).then_inc(w_parts, 1)

                def store(u):
                    act.wait_ge(w_tr, u + 1)
                    dst = (wgu_t[:, :, u * 512:(u + 1) * 512] if u < NGU else
                           wp_t[:, :, (u - NGU) * P:(u - NGU + 1) * P])
                    act.activation(dst, ps_w[u % 2][:, :].bitcast(BF16).rearrange("p (a b) -> p a b", a=dst.shape[1]),
                                   ACT.Copy).then_inc(w_st, 1)

                for u in range(NTU + 2):
                    if u < NTU:
                        parts(u)
                    if u >= 2:
                        store(u - 2)

            def attention_weight(m):
                act.wait_ge(a_tr, m + 1)
                act.wait_ge(sc_step, 7)
                for half in (0, 1):
                    act.activation(wat_hi[m][:, 2 * half:2 * half + 2, :],
                                   ps_w[half][:, :].rearrange("p (k d) -> p k d", k=2), ACT.Copy,
                                   scale=w_scale[:, m:m + 1]).then_inc(a_hi, 1)

            def copy_hi(dst, src, ready, n, done, scale=1.0):
                act.wait_ge(ready, n)
                act.activation(dst, src, ACT.Copy, scale=scale).then_inc(done, 1)

            def xt_piece(s, b):
                copy_hi(xt_hi[s][:, :, :].rearrange("p a b -> p (a b)"), ps_m[:, :], p_xt[s], b + 1, a_xt[s])

            def half_tanh(s, b, c, n):
                act.wait_ge(p_up[s], 8 * b + 2 * c + 1)
                act.activation(gate[:, n, :], ps_gu[:, 0:CH], ACT.Tanh, scale=0.5 * 2.0 ** -XS_LOG2)\
                   .then_inc(a_tanh[s], 1)

            def square(s, b, c, n):
                act.wait_ge(d_h[s], 4 * b + c + 1)
                act.activation(gate[:, n, :], h[s][:, c * CH:(c + 1) * CH], ACT.Square,
                               accum_out=sq_parts[s][:, c:c + 1]).then_inc(a_sq[s], 1)

            def exps(b, q, place):
                act.wait_ge(d_bias, 8 * b + q + 1)
                keys = slice(0 if place else P, 2 * P)
                for j in range(4):
                    hd = 4 * q + j
                    p = prob[:, q % 2, j, keys]
                    e = act.activation(p, p, ACT.Exp, bias=exp_bias[:, hd:hd + 1], scale=exp_scale[:, 0:1],
                                       accum_out=row_sum[:, hd:hd + 1])
                e.then_inc(a_exp, 1)

            def prob_hi(b, q, banks, place):
                for pair in range(2):
                    copy_hi(prob_t_view(pt_hi[:, 4 * pair:4 * pair + 4, :], place), ps_t_view(banks[pair], place),
                            p_pt, 16 * b + 2 * q + pair + 1, a_pt)

            def head_view(ap):
                return ap.rearrange("p (h d) -> p h d", d=DK)

            def body(i, place):
                bL, bA, bQ, bT, bW, bE = i + 1, i, i - 1, i - 2, i - 3, i - 4
                for hs in range(8):
                    up, bu = ("A", bA) if hs < 4 else ("C", bW)
                    dn, bd = ("C", bE) if hs < 4 else ("A", bA)
                    c = hs % 4
                    bp, qp, p_place = (bW, 7, place - 3) if hs < 1 else (bT, hs - 1, place - 2)
                    p_place %= BPS
                    if isinstance(i, int) and i == 0 and hs >= 5:
                        attention_weight(hs - 5)
                    if on(bp):
                        exps(bp, qp, p_place)
                    if hs == 1 and on(bQ):
                        act.wait_ge(p_q, bQ + 1)
                        act.activation(qk4[:, :, 0, :], head_view(ps_m[:, :]), ACT.Copy,
                                       scale=2.0 ** -DOWN_LOG2).then_inc(a_q, 1)
                    if hs == 4 and on(bQ):
                        act.wait_ge(p_k, bQ + 1)
                        act.activation(qk4[:, :, 0, :], head_view(ps_m[:, :]), ACT.Copy,
                                       scale=2.0 ** -DOWN_LOG2).then_inc(a_k, 1)
                    if on(bu):
                        half_tanh(up, bu, c, hs % 2)
                    if on(bd):
                        copy_hi(ht_hi[:, c % 2, :, :].rearrange("p a b -> p (a b)"), ps_ht[:, :],
                                p_ht[dn], 4 * bd + c + 1, a_ht[dn])
                    if hs == 0 and on(bQ):
                        xt_piece("B", bQ)
                    if hs == 2 and on(bW):
                        copy_hi(ot_hi[:, :, :].rearrange("p a b -> p (a b)"), ps_m[:, :], p_ot, bW + 1, a_ot)
                    if hs == 3 and on(bW):
                        xt_piece("C", bW)
                    if on(bp):
                        prob_hi(bp, qp, pt_banks(i, hs), p_place)
                    if hs == 4 and on(bQ):
                        copy_hi(kt[:, 0:8, (place - 1) % BPS, :], ps_m16, p_kt, 2 * bQ + 1, a_kt)
                    if hs == 5 and on(bQ):
                        copy_hi(kt[:, 8:16, (place - 1) % BPS, :], ps_m16, p_kt, 2 * bQ + 2, a_kt)
                    if hs == 6 and on(bL):
                        xt_piece("A", bL)
                    if on(bu):
                        square(up, bu, c, hs % 2)
                    if hs == 7 and on(bQ):
                        act.wait_ge(p_v, bQ + 1)
                        act.activation(v[:, (place - 1) % BPS, :, 0, :], head_view(ps_m[:, :]), ACT.Copy,
                                       scale=2.0 ** -DOWN_LOG2).then_inc(a_v, 1)
                if isinstance(i, int) and i == 0:
                    attention_weight(3)

            all_iterations(act, body, ternary_weights)

        @block.vector
        def _(dve):
            def hold():
                dve.memset(place_of_carrier(), 0.0)

            dve.wait_ge(consts, NCONST)
            dve.tensor_copy(id16[:, :], id32[:, :]).then_inc(ids, 1)
            dve.tensor_copy(idb[:, :], id32[:, :]).then_inc(ids, 1)

            def ternary_weights():
                def scales(u):
                    n = u % 2
                    dve.wait_ge(w_parts, u + 1)
                    dve.tensor_reduce(grp_sum[:, n, :], w_abs[u % 3].rearrange("p (g k) -> p g k", g=G64), AX.X,
                                      ALU.add).then_inc(w_sum, 1)
                    dve.wait_ge(w_sum, u + 1)
                    need(dve, w_dif, u - 1)
                    dve.tensor_scalar(grp_scale[:, n, :], grp_sum[:, n, :], 1.0 / 64, CLIP_MIN,
                                      ALU.mult, ALU.max).then_inc(w_grp, 1)

                def quantise(u):
                    n, m = u % 2, u % 3
                    dve.wait_ge(w_dif, u + 1)
                    dve.tensor_tensor(out=w_keep, in0=w_abs[m], in1=w_diff[n], op=ALU.is_gt).then_inc(w_kp, 1)
                    dve.wait_ge(w_kp, u + 1)
                    dve.tensor_tensor(out=w_diff[n], in0=w_abs[m], in1=w_diff[n], op=ALU.add).then_inc(w_step, 1)
                    dve.wait_ge(w_step, 2 * u + 1)
                    dve.tensor_tensor(out=w_diff[n], in0=w_diff[n], in1=w_keep, op=ALU.mult).then_inc(w_step, 1)
                    dve.wait_ge(w_step, 2 * u + 2)
                    need(dve, w_tr, u - 1)
                    dve.tensor_tensor(out=w_tern[n], in0=w_diff[n], in1=w_sign[m], op=ALU.mult).then_inc(w_q, 1)

                for u in range(NTU + 1):
                    if u < NTU:
                        scales(u)
                    if u > 0:
                        quantise(u - 1)

            def largest(m):
                dve.wait_ge(a_in[m], 16)
                dve.tensor_reduce(w_absmax[:, m:m + 1], at_raw[m], AX.XY, ALU.max,
                                  apply_absolute_value=True).then_inc(a_mx, 1)

            def attention_scales():
                dve.wait_ge(a_all, 1)
                dve.tensor_scalar(w_floor[:, :], w_max[:, :], 2.0 ** -40, None, ALU.max).then_inc(sc_step, 1)
                dve.wait_ge(sc_step, 1)
                dve.tensor_scalar(w_pow2[:, :].bitcast(U32), w_floor[:, :].bitcast(U32), 0x7F800000, None,
                                  ALU.bitwise_and).then_inc(sc_step, 1)
                dve.wait_ge(sc_step, 2)
                dve.reciprocal(w_rec[:, :], w_pow2[:, :]).then_inc(sc_step, 1)
                dve.wait_ge(sc_step, 3)
                dve.tensor_scalar(w_scale[:, :], w_rec[:, :], 2.0 ** WS_LOG2, None, ALU.mult).then_inc(sc_step, 1)
                dve.tensor_scalar(exp_scale[:, :], w_pow2[:, Q:Q + 1], w_pow2[:, K:K + 1],
                                  2.0 ** -10 / math.sqrt(DK), ALU.mult, ALU.mult).then_inc(sc_step, 1)
                dve.tensor_scalar(out_scale[:, :], w_pow2[:, V:V + 1], w_pow2[:, O:O + 1],
                                  2.0 ** -(5 + WS_LOG2), ALU.mult, ALU.mult).then_inc(sc_step, 1)
                dve.wait_ge(sc_step, 6)
                dve.tensor_scalar(neg_exp_scale[:, :], exp_scale[:, :], -1.0, None, ALU.mult).then_inc(sc_step, 1)
                dve.wait_ge(sc_step, 7)

            def attention_weight(m):
                for half in (0, 1):
                    k = slice(2 * half, 2 * half + 2)
                    dve.wait_ge(a_hi, 2 * m + half + 1)
                    dve.scalar_tensor_tensor(out=wat_lo[m][:, k, :],
                                             in0=ps_w[half][:, :].rearrange("p (k d) -> p k d", k=2),
                                             scalar=w_scale[:, m:m + 1], in1=wat_hi[m][:, k, :], op0=ALU.mult,
                                             op1=ALU.subtract).then_inc(a_lo, 1)

            def flat(ap):
                return ap.rearrange("p a b -> p (a b)")

            def head_view(ap):
                return ap.rearrange("p (h d) -> p h d", d=DK)

            def norm_stats(s, b, ready, n, scale):
                dve.wait_ge(ready, n)
                hold()
                dve.bn_stats(st6[s][:, :], slot(b)).then_inc(d_st[s], 1)
                dve.wait_ge(d_st[s], b + 1)
                hold()
                dve.bn_aggr(mean_var[s][:, :], st6[s][:, :]).then_inc(d_mv[s], 1)
                dve.wait_ge(d_mv[s], b + 1)
                dve.tensor_scalar(var_eps[s][:, :], mean_var[s][:, 1:2], LN_EPS, scale, ALU.add, ALU.mult)\
                   .then_inc(d_ve[s], 1)

            def norm_apply(s, b):
                dve.wait_ge(g_rstd[s], b + 1)
                dve.tensor_scalar(xhat[:, :], slot(b), mean_var[s][:, 0:1], rstd[s][:, 0:1],
                                  ALU.subtract, ALU.mult).then_inc(d_xh[s], 1)

            def rms_stats(s, b):
                dve.wait_ge(a_sq[s], 4 * b + 4)
                dve.tensor_reduce(sq_sum[s][:, :], sq_parts[s][:, :], AX.X, ALU.add).then_inc(d_sqs[s], 1)
                dve.wait_ge(d_sqs[s], b + 1)
                down = 2.0 ** (-2 * HS_LOG2)
                dve.tensor_scalar(sq_mean[s][:, :], sq_sum[s][:, :], down / H, down * RMS_EPS,
                                  ALU.mult, ALU.add).then_inc(d_sqm[s], 1)

            def rms_apply(s, b, rest):
                at = slice(CH, H) if rest else slice(0, CH)
                dve.wait_ge(g_rms[s], b + 1)
                dve.tensor_scalar(h[s][:, at], h[s][:, at], rms_inv[s][:, 0:1], None, ALU.mult).then_inc(d_hn[s], 1)

            def masked_max(b, q, place):
                dve.wait_ge(p_s, 8 * b + q + 1)
                hold()
                first = 0 if place else P
                for pair in range(2):
                    for o in range(2):
                        hd = 4 * q + 2 * pair + o
                        at = o * CH + pair * 2 * P
                        m = dve.tensor_tensor_reduce(prob[:, q % 2, 2 * pair + o, first:2 * P],
                                                     ps_s[:, at + first:at + 2 * P], mask[:, first:2 * P],
                                                     1.0, NEG, ALU.add, ALU.max, row_max[:, hd:hd + 1])
                m.then_inc(d_mx, 1)
                dve.wait_ge(d_mx, 8 * b + q + 1)
                dve.tensor_scalar(exp_bias[:, 4 * q:4 * q + 4], row_max[:, 4 * q:4 * q + 4], neg_exp_scale[:, 0:1],
                                  PROB_LOG2 * math.log(2.0), ALU.mult, ALU.add).then_inc(d_bias, 1)

            def gated(s, b, c, n):
                dve.wait_ge(a_tanh[s], 4 * b + c + 1)
                dve.scalar_tensor_tensor(out=gate[:, n, :], in0=gate[:, n, :], scalar=1.0, in1=ps_gu[:, 0:CH],
                                         op0=ALU.add, op1=ALU.mult).then_inc(d_gate[s], 1)

            def hidden(s, b, c, n):
                dve.wait_ge(d_gate[s], 4 * b + c + 1)
                dve.wait_ge(p_up[s], 8 * b + 2 * c + 2)
                dve.scalar_tensor_tensor(out=h[s][:, c * CH:(c + 1) * CH], in0=ps_gu[:, CH:2 * CH],
                                         scalar=0.5 * 2.0 ** (-2 * XS_LOG2), in1=gate[:, n, :], op0=ALU.mult,
                                         op1=ALU.mult).then_inc(d_h[s], 1)

            def take_lo(dst, src, hi, ready, n, done):
                dve.wait_ge(ready, n)
                dve.tensor_tensor(out=dst, in0=src, in1=hi, op=ALU.subtract).then_inc(done, 1)

            def prob_lo(b, q, banks, place):
                for pair in range(2):
                    tiles = slice(4 * pair, 4 * pair + 4)
                    take_lo(prob_t_view(pt_lo[:, tiles, :], place), ps_t_view(banks[pair], place),
                            prob_t_view(pt_hi[:, tiles, :], place), a_pt, 16 * b + 2 * q + pair + 1, d_pt)

            def normalise_o(b, ct):
                dve.wait_ge(p_pv, 8 * b + 2 * ct + 2)
                o = ps_o[:, 0:8 * 3 * DK].rearrange("p (h t d) -> p h d t", h=8, t=3)
                dve.tensor_reduce(o_sum[:, :, :], o, AX.X, ALU.add).then_inc(d_osum, 1)
                dve.reciprocal(row_inv[:, :], row_sum[:, 8 * ct:8 * ct + 8]).then_inc(d_rinv, 1)
                dve.wait_ge(d_osum, 4 * b + ct + 1)
                dve.wait_ge(d_rinv, 4 * b + ct + 1)
                dve.tensor_tensor(out=head_view(o_norm[:, ct * P:(ct + 1) * P]), in0=o_sum[:, :, :],
                                  in1=row_inv[:, :].unsqueeze(2).to_broadcast([P, 8, DK]),
                                  op=ALU.mult).then_inc(d_on, 1)

            def add_ffn(s, b, done):
                dve.wait_ge(p_dn[s], 4 * b + 4)
                dve.scalar_tensor_tensor(out=slot(b), in0=ps_y[:, :], scalar=0.5 * 2.0 ** -HS_LOG2, in1=slot(b),
                                         op0=ALU.mult, op1=ALU.add).then_inc(done, 1)

            def body(i, place):
                bL, bA, bQ, bT, bW, bE = i + 1, i, i - 1, i - 2, i - 3, i - 4
                for hs in range(8):
                    up, bu = ("A", bA) if hs < 4 else ("C", bW)
                    dn, bd = ("C", bE) if hs < 4 else ("A", bA)
                    c = hs % 4
                    bp, qp, p_place = (bW, 7, place - 3) if hs < 1 else (bT, hs - 1, place - 2)
                    p_place %= BPS
                    bv, qv, v_place = (bW, hs + 6, place - 3) if hs < 2 else (bT, hs - 2, place - 2)
                    v_place %= BPS
                    if isinstance(i, int) and i == 0:
                        if hs < 4:
                            largest(hs)
                        elif hs == 4:
                            attention_scales()
                        else:
                            attention_weight(hs - 5)
                    if hs == 0 and on(bQ):
                        norm_stats("B", bQ, d_x1, bQ + 1, 2.0 ** (-2 * XS_LOG2))
                    if hs == 1 and on(bL):
                        odd = (place + 1) % 2
                        norm_stats("A", bL, x_in[odd], 8 * (bL - odd) + 16, 2.0 ** (-2 * XS_LOG2))
                    if hs == 1 and on(bQ):
                        dve.wait_ge(a_q, bQ + 1)
                        dve.scalar_tensor_tensor(out=qk4[:, :, 1, :], in0=head_view(ps_m[:, :]),
                                                 scalar=2.0 ** -DOWN_LOG2, in1=qk4[:, :, 0, :], op0=ALU.mult,
                                                 op1=ALU.subtract).then_inc(d_qlo, 1)
                        dve.wait_ge(d_qlo, bQ + 1)
                        dve.tensor_copy(qk4[:, :, 2:4, :], qk4[:, :, 0:2, :]).then_inc(d_q, 1)
                    if hs == 3 and on(bW):
                        dve.wait_ge(p_wo, bW + 1)
                        dve.scalar_tensor_tensor(out=slot(bW), in0=ps_m[:, :], scalar=out_scale[:, 0:1],
                                                 in1=slot(bW), op0=ALU.mult, op1=ALU.add).then_inc(d_x2, 1)
                        norm_stats("C", bW, d_x2, bW + 1, 2.0 ** (-2 * XS_LOG2))
                    if hs == 4 and on(bQ):
                        k4 = qk4[:, :, :, :].rearrange("p h (a b) d -> p h a b d", b=2)
                        dve.wait_ge(a_k, bQ + 1)
                        dve.scalar_tensor_tensor(out=qk4[:, :, 2, :], in0=head_view(ps_m[:, :]),
                                                 scalar=2.0 ** -DOWN_LOG2, in1=qk4[:, :, 0, :], op0=ALU.mult,
                                                 op1=ALU.subtract).then_inc(d_klo, 1)
                        dve.wait_ge(d_klo, bQ + 1)
                        dve.tensor_copy(k4[:, :, :, 1, :], k4[:, :, :, 0, :]).then_inc(d_k, 1)
                    if on(bT):
                        masked_max(bT, hs, (place - 2) % BPS)
                    if hs == 2 and on(bQ):
                        dve.wait_ge(p_qt, 2 * bQ + 2)
                        dve.tensor_copy(qt[:, (place - 1) % 2, 8:16, :], ps_m16).then_inc(d_qt, 1)
                    if hs == 0 and on(bQ):
                        need(dve, p_xt["A"], last(i) + 1)
                        norm_apply("B", bQ)
                    if hs == 3 and on(bW):
                        if on(bQ):
                            dve.wait_ge(p_xt["B"], bQ + 1)
                        else:
                            dve.wait_ge(p_xt["C"], bW)
                        norm_apply("C", bW)
                    if on(bu):
                        gated(up, bu, c, hs % 2)
                        if hs not in (0, 3):
                            hidden(up, bu, c, hs % 2)
                    if on(bd):
                        take_lo(flat(ht_lo[:, c % 2, :, :]), ps_ht[:, :], flat(ht_hi[:, c % 2, :, :]),
                                a_ht[dn], 4 * bd + c + 1, d_ht[dn])
                    if on(bu) and hs in (0, 3):
                        hidden(up, bu, c, hs % 2)
                    if hs == 0 and on(bQ):
                        take_lo(flat(xt_lo["B"][:, :, :]), ps_m[:, :], flat(xt_hi["B"][:, :, :]),
                                a_xt["B"], bQ + 1, d_xt["B"])
                    if hs == 2 and on(bW):
                        take_lo(flat(ot_lo[:, :, :]), ps_m[:, :], flat(ot_hi[:, :, :]), a_ot, bW + 1, d_ot)
                    if hs == 3 and on(bW):
                        take_lo(flat(xt_lo["C"][:, :, :]), ps_m[:, :], flat(xt_hi["C"][:, :, :]),
                                a_xt["C"], bW + 1, d_xt["C"])
                    if on(bp):
                        prob_lo(bp, qp, pt_banks(i, hs), p_place)
                    if hs == 1 and on(bQ):
                        dve.wait_ge(p_qt, 2 * bQ + 1)
                        dve.tensor_copy(qt[:, (place - 1) % 2, 0:8, :], ps_m16).then_inc(d_qt, 1)
                    if hs == 6 and on(bL):
                        take_lo(flat(xt_lo["A"][:, :, :]), ps_m[:, :], flat(xt_hi["A"][:, :, :]),
                                a_xt["A"], bL + 1, d_xt["A"])
                    if hs == 3 and on(bA):
                        rms_stats("A", bA)
                    if hs == 7 and on(bW):
                        rms_stats("C", bW)
                    if hs % 2 and on(bv):
                        normalise_o(bv, qv // 2)
                    if hs == 3 and on(bE):
                        add_ffn("C", bE, d_x3)
                    if hs == 3 and on(bA):
                        rms_apply("A", bA, False)
                    if hs == 4 and on(bA):
                        rms_apply("A", bA, True)
                    if hs == 5 and on(bL):
                        if on(bW):
                            dve.wait_ge(p_xt["C"], bW + 1)
                        elif on(bQ):
                            dve.wait_ge(p_xt["B"], bQ + 1)
                        else:
                            need(dve, p_xt["A"], bL)
                        norm_apply("A", bL)
                    if hs == 7 and on(bA):
                        add_ffn("A", bA, d_x1)
                    if hs == 7 and on(bW):
                        rms_apply("C", bW, False)
                    if hs == 7 and on(bQ):
                        dve.wait_ge(a_v, bQ + 1)
                        need(dve, g_v, bQ)
                        dve.scalar_tensor_tensor(out=head_view(v_rest[:, :]), in0=head_view(ps_m[:, :]),
                                                 scalar=2.0 ** -DOWN_LOG2, in1=v[:, (place - 1) % BPS, :, 0, :],
                                                 op0=ALU.mult, op1=ALU.subtract).then_inc(d_v, 1)
                    if hs == 0 and on(bE):
                        rms_apply("C", bE, True)
                if isinstance(i, int) and i == 0:
                    attention_weight(3)

            all_iterations(dve, body, ternary_weights)

        @block.tensor
        def _(pe):
            pe.wait_ge(ids, 2)

            def ternary_weights():
                for u in range(NTU):
                    pe.wait_ge(w_q, u + 1)
                    need(pe, w_st, u - 1)
                    bank = ps_w[u % 2][:, :].bitcast(BF16)
                    for a in range(4):
                        for k in range(4):
                            if u < NGU:
                                src, dst = a * 512 + k * P, k * 512 + a * P
                            else:
                                src = dst = (4 * a + k) * P
                            t = pe.transpose(bank[:, dst:dst + P], w_tern[u % 2][:, src:src + P], idb[:, :])
                    t.then_inc(w_tr, 1)

            def attention_weight(m):
                pe.wait_ge(a_in[m], 16)
                need(pe, a_hi, 2 * m)
                need(pe, a_lo, 2 * m)
                for k in range(4):
                    for a in range(4):
                        at = (k % 2) * 512 + a * P
                        t = pe.transpose(ps_w[k // 2][:, at:at + P], at_raw[m][:, a, k * P:(k + 1) * P], id32[:, :])
                t.then_inc(a_tr, 1)

            def xt_piece(s, b):
                pe.wait_ge(d_xh[s], b + 1)
                for k in range(KD):
                    t = pe.transpose(ps_m[:, k * P:(k + 1) * P], xhat[:, k * P:(k + 1) * P], id32[:, :])
                t.then_inc(p_xt[s], 1)

            def up(s, b, c):
                for half in (0, 1):
                    n = 0
                    for k in range(KD):
                        for part in (xt_hi[s], xt_lo[s]):
                            t = pe.matmul(ps_gu[:, half * CH:(half + 1) * CH], part[:, k, :],
                                          wgu_t[:, k, half * H + c * CH:half * H + (c + 1) * CH],
                                          start=(n == 0), stop=(n == 2 * KD - 1))
                            n += 1
                    t.then_inc(p_up[s], 1)

            def hidden_t(s, b, g):
                for j in range(4):
                    at = (4 * g + j) * P
                    t = pe.transpose(ps_ht[:, j * P:(j + 1) * P], h[s][:, at:at + P], id32[:, :])
                t.then_inc(p_ht[s], 1)

            def down(s, b, g):
                for part, ready in ((ht_hi, a_ht[s]), (ht_lo, d_ht[s])):
                    pe.wait_ge(ready, 4 * b + g + 1)
                    for j in range(4):
                        t = pe.matmul(ps_y[:, :], part[:, g % 2, j, :], wp_t[:, 4 * g + j, :],
                                      start=(g == 0 and j == 0 and part is ht_hi),
                                      stop=(g == 3 and j == 3 and part is ht_lo))
                t.then_inc(p_dn[s], 1)

            def project(m, hi, lo, done, ks=range(KD)):
                for k in ks:
                    for n, (part, w) in enumerate(((hi, wat_hi), (hi, wat_lo), (lo, wat_hi))):
                        t = pe.matmul(ps_m[:, :], part[:, k, :], w[m][:, k, :], start=(k == 0 and n == 0),
                                      stop=(k == KD - 1 and n == 2))
                if ks[-1] == KD - 1:
                    t.then_inc(done, 1)

            def heads_t(f, done):
                for j in range(8):
                    pair = 8 * f + j
                    t = pe.transpose(ps_m16[:, j, :],
                                     qk4[:, 2 * pair:2 * pair + 2, :, :].rearrange("p a b c -> p (a b c)"), id16[:, :])
                t.then_inc(done, 1)

            def scores(b, q, place):
                for pair in range(2):
                    for o in range(2):
                        at = o * CH + pair * 2 * P
                        rows = slice(64 * o, 64 * o + 64)
                        if place:
                            out_at, keys = slice(at, at + 2 * P), slice(place - 1, place + 1)
                        else:
                            out_at, keys = slice(at + P, at + 2 * P), slice(0, 1)
                        t = pe.matmul(ps_s[:, out_at], qt[rows, place % 2, 2 * q + pair, :],
                                      kt[rows, 2 * q + pair, keys, :].rearrange("p a b -> p (a b)"),
                                      start=True, stop=True)
                t.then_inc(p_s, 1)

            def prob_t(b, q, banks, place):
                pe.wait_ge(a_exp, 8 * b + q + 1)
                for pair in range(2):
                    for j in (2 * pair, 2 * pair + 1):
                        for half in ((0, 1) if place else (1,)):
                            at = (2 * j + half) % 4 * P
                            t = pe.transpose(banks[pair][:, at:at + P], prob[:, q % 2, j, half * P:(half + 1) * P],
                                             id32[:, :])
                    t.then_inc(p_pt, 1)

            def prob_v(b, q, place):
                pe.wait_ge(d_pt, 16 * b + 2 * q + 2)
                for j in range(4):
                    hd = 4 * q + j
                    at = (hd % 8) * 3 * DK
                    products = [(half, part) for half in ((0, 1) if place else (1,)) for part in (pt_hi, pt_lo)]
                    for n, (half, part) in enumerate(products):
                        t = pe.matmul(ps_o[:, at:at + 3 * DK], part[:, 2 * j + half, :],
                                      v[:, place - 1 + half, hd, :, :].rearrange("p a b -> p (a b)"),
                                      start=(n == 0), stop=(n == len(products) - 1))
                t.then_inc(p_pv, 1)

            def body(i, place):
                bL, bA, bQ, bT, bW, bE = i + 1, i, i - 1, i - 2, i - 3, i - 4
                for hs in range(8):
                    c = hs % 4
                    bp, qp, p_place = (bW, 7, place - 3) if hs < 1 else (bT, hs - 1, place - 2)
                    p_place %= BPS
                    bv, qv, v_place = (bW, hs + 6, place - 3) if hs < 2 else (bT, hs - 2, place - 2)
                    v_place %= BPS
                    if isinstance(i, int) and i == 0 and hs >= 4:
                        if hs == 4:
                            pe.wait_ge(d_h["A"], 4)
                        attention_weight(hs - 4)
                    if hs == 1 and on(bQ):
                        pe.wait_ge(d_xt["B"], bQ + 1)
                        project(Q, xt_hi["B"], xt_lo["B"], p_q)
                    if hs == 3 and on(bW):
                        pe.wait_ge(d_ot, bW + 1)
                        project(O, ot_hi, ot_lo, p_wo)
                    if hs == 4 and on(bQ):
                        if on(bW):
                            pe.wait_ge(d_xt["C"], bW + 1)
                        else:
                            pe.wait_ge(d_qt, 2 * bQ + 2)
                        project(K, xt_hi["B"], xt_lo["B"], p_k)
                    if on(bT):
                        if hs == 0:
                            pe.wait_ge(d_qt, 2 * bT + 2)
                            pe.wait_ge(a_kt, 2 * bT + 2)
                        if spare(i, hs - 1) if hs else isinstance(i, int) and spare(i - 1, 7):
                            need(pe, d_bias, 8 * bT + hs)
                        else:
                            need(pe, d_pt, 16 * bT + 2 * (hs - 1))
                        scores(bT, hs, (place - 2) % BPS)
                    if hs == 2 and on(bQ):
                        pe.wait_ge(d_qt, 2 * bQ + 1)
                        heads_t(1, p_qt)
                    if hs == 4 and on(bT) and spare(i, 3):
                        pe.wait_ge(d_pt, 16 * bT + 6)
                    if hs == 4 and spare(i, 3) and not on(bT) and on(bW):
                        pe.wait_ge(d_pt, 16 * NB)
                    if hs == 0 and on(bW) and isinstance(i, int) and spare(i - 1, 7):
                        pe.wait_ge(d_pt, 16 * bW + 14)
                    if hs < 4 and on(bA):
                        if hs == 0:
                            pe.wait_ge(d_xt["A"], bA + 1)
                            need(pe, d_h["C"], 4 * (i - 4) + 4)
                            if isinstance(i, int) and i - 4 < 0:
                                need(pe, d_h["A"], 4 * bA)
                        else:
                            pe.wait_ge(d_h["A"], 4 * bA + c)
                        up("A", bA, c)
                    if hs >= 4 and on(bW):
                        if hs == 4:
                            pe.wait_ge(d_xt["C"], bW + 1)
                            pe.wait_ge(d_h["A"], 4 * last(i) + 4)
                            need(pe, d_h["C"], 4 * bW)
                        else:
                            pe.wait_ge(d_h["C"], 4 * bW + c)
                        up("C", bW, c)
                    if hs < 4 and on(bE):
                        if hs == 0:
                            pe.wait_ge(d_hn["C"], 2 * bE + 1)
                            pe.wait_ge(d_ht["A"], 4 * last(i - 1) + 4)
                            need(pe, d_ht["C"], 4 * bE)
                        else:
                            pe.wait_ge(d_ht["C"], 4 * bE + c)
                            pe.wait_ge(d_hn["C"], 2 * bE + 2)
                        hidden_t("C", bE, c)
                    if hs >= 4 and on(bA):
                        if hs == 4:
                            pe.wait_ge(d_hn["A"], 2 * bA + 1)
                            need(pe, d_ht["C"], 4 * (i - 4) + 4)
                            need(pe, d_ht["A"], 4 * bA)
                        else:
                            pe.wait_ge(d_ht["A"], 4 * bA + c)
                            pe.wait_ge(d_hn["A"], 2 * bA + 2)
                        hidden_t("A", bA, c)
                    if on(bv):
                        if qv == 0:
                            pe.wait_ge(g_v, bv + 1)
                        if qv % 2 == 0:
                            need(pe, d_on, 4 * bv + qv // 2)
                        prob_v(bv, qv, v_place)
                    if on(bp):
                        if spare(i, hs):
                            need(pe, d_pt, 16 * bp + 2 * qp)
                            if spare(i, hs) == "gu":
                                need(pe, d_h["A"], 4 * last(i if hs >= 4 else i - 1) + 4)
                                need(pe, d_h["C"], 4 * (i - 4) + 4)
                            else:
                                need(pe, d_ht["A"], 4 * last(i - 1) + 4)
                                need(pe, d_x1, last(i - 1) + 1)
                                need(pe, d_ht["C"], 4 * (i - 4 if hs >= 4 else i - 5) + 4)
                                need(pe, d_x3, i - 3 if hs >= 4 else i - 4)
                        else:
                            pe.wait_ge(d_bias, 8 * bT + hs + 1)
                        prob_t(bp, qp, pt_banks(i, hs), p_place)
                    if hs == 0 and on(bQ):
                        pe.wait_ge(d_xt["A"], last(i) + 1)
                        need(pe, d_v, bQ)
                        xt_piece("B", bQ)
                    if hs == 1 and on(bQ):
                        pe.wait_ge(d_q, bQ + 1)
                        heads_t(0, p_qt)
                    if hs == 2 and on(bW):
                        if on(bQ):
                            pe.wait_ge(d_qt, 2 * bQ + 2)
                        else:
                            pe.wait_ge(d_v, NB)
                            pe.wait_ge(d_xt["C"], bW)
                        pe.wait_ge(d_on, 4 * bW + 4)
                        for k in range(KD):
                            t = pe.transpose(ps_m[:, k * P:(k + 1) * P], o_norm[:, k * P:(k + 1) * P], id32[:, :])
                        t.then_inc(p_ot, 1)
                    if hs == 3 and on(bW):
                        xt_piece("C", bW)
                    if hs == 4 and on(bQ):
                        pe.wait_ge(d_k, bQ + 1)
                        heads_t(0, p_kt)
                    if hs == 5 and on(bQ):
                        pe.wait_ge(a_kt, 2 * bQ + 1)
                        heads_t(1, p_kt)
                    if hs == 6 and on(bL):
                        if on(bQ):
                            pe.wait_ge(a_kt, 2 * bQ + 2)
                        else:
                            need(pe, d_xt["A"], bL)
                        xt_piece("A", bL)
                    if hs == 7 and on(bQ):
                        if on(bL):
                            pe.wait_ge(d_xt["A"], bL + 1)
                        else:
                            pe.wait_ge(a_kt, 2 * bQ + 2)
                        project(V, xt_hi["B"], xt_lo["B"], p_v, range(0, KD // 2))
                    if hs < 4 and on(bE):
                        if hs == 0:
                            pe.wait_ge(d_x1, last(i - 1) + 1)
                            need(pe, d_x3, bE)
                        down("C", bE, c)
                    if hs >= 4 and on(bA):
                        if hs == 4:
                            need(pe, d_x3, i - 3)
                            need(pe, d_x1, bA)
                        down("A", bA, c)
                    if hs == 7 and on(bQ):
                        project(V, xt_hi["B"], xt_lo["B"], p_v, range(KD // 2, KD))

            all_iterations(pe, body, ternary_weights)
_INS=['L0_attn_x','L0_attn_Wq','L0_attn_Wk','L0_attn_Wv','L0_attn_Wo','L0_ffn_w_gate_up','L0_ffn_w_proj']
def kernel(**inputs):
    import numpy as _np
    import concourse.bacc as _bacc
    from concourse import mybir as _mybir
    from concourse.bass_utils import run_bass_kernel_spmd as _run
    nc=_bacc.Bacc("TRN2",target_bir_lowering=False,num_devices=1)
    arrays,args={},[]
    for name in _INS:
        a=_np.ascontiguousarray(inputs[name])
        arrays[f"in_{name}_dram"]=a
        args.append(nc.dram_tensor(f"in_{name}_dram",a.shape,_mybir.dt.from_np(a.dtype),kind="ExternalInput").ap())
    args.append(nc.dram_tensor("out_0_dram",(8,512,512),_mybir.dt.float32,kind="ExternalOutput").ap())
    macaron(nc,*args)
    r=_run(nc,[arrays],core_ids=[0])
    return r.results[0]["out_0_dram"]
```

```python
from contextlib import ExitStack
import math

import concourse.bass as bass
from concourse import mybir

F32 = mybir.dt.float32
F16 = mybir.dt.float16
BF16 = mybir.dt.bfloat16
U32 = mybir.dt.uint32
ALU = mybir.AluOpType
ACT = mybir.ActivationFunctionType
AX = mybir.AxisListType
RMAX = bass.bass_isa.ReduceOp.max

P = 128
HEADS = 32
LN_EPS = 1e-5
RMS_EPS = 2.0 ** -23
CLIP_MIN = 1.0011717677116394e-08
NEG = -3.0e38
PROB_LOG2 = 15


def macaron(nc, x, Wq, Wk, Wv, Wo, w_gate_up, w_proj, out):
    B, S, D = x.shape
    H = w_proj.shape[1]
    KD, KH = D // P, H // P
    DK = D // HEADS
    NB = B * S // P
    BPS = S // P
    CH = 512
    NC = H // CH
    XS_LOG2 = 11
    WS_LOG2 = 13
    DOWN_LOG2 = XS_LOG2 + WS_LOG2 - 5
    HS_LOG2 = 10
    RING = 7
    assert D == 512 and H == 2048 and DK == 16 and NC == 4

    xf = x.rearrange("b t d -> (b t) d")
    of = out.rearrange("b t d -> (b t) d")
    gu_units = w_gate_up.rearrange("(u t p) d -> u p t d", t=4, p=P)
    wp_units = w_proj.rearrange("(u p) h -> u p h", p=P)
    at_units = [w.rearrange("(t p) d -> p t d", p=P) for w in (Wq, Wk, Wv, Wo)]
    NGU, NWP = 2 * H // 512, D // P
    NTU = NGU + NWP
    G64 = 32
    UNITS = [u for c in range(NC) for u in (c, NC + c)] + list(range(NGU, NTU))

    with ExitStack() as ctx:
        def sb(name, shape, dt):
            return ctx.enter_context(nc.sbuf_tensor(name, shape, dt))

        def psum(name, shape):
            return ctx.enter_context(nc.psum_tensor(name, shape, F32))

        def sem(name):
            return ctx.enter_context(nc.semaphore(name))

        ps_s = psum("ps_s", [P, 1024])
        ps_gu = psum("ps_gu", [P, 1024])
        ps_y = psum("ps_y", [P, CH])
        ps_ht = psum("ps_ht", [P, CH])
        ps_o = psum("ps_o", [P, CH])
        ps_m = psum("ps_m", [P, CH])
        ps_m16 = ps_m[:, :].bitcast(F16).rearrange("p (a b) -> p a b", b=P)

        wgu_t = sb("wgu_t", [P, KD, 2 * H], BF16)
        wp_t = sb("wp_t", [P, KH, D], BF16)
        wat_hi = [sb(f"w{n}_hi", [P, KD, D], F16) for n in "qkvo"]
        wat_lo = [sb(f"w{n}_lo", [P, KD, D], F16) for n in "qkvo"]
        Q, K, V, O = range(4)
        stream = sb("stream", [P, RING, D], F32)
        xhat = sb("xhat", [P, D], F32)
        v_rest = sb("v_rest", [P, D], F32)
        xt_hi = {s: sb(f"xt_hi_{s}", [P, KD, P], F16) for s in "ABC"}
        xt_lo = {s: sb(f"xt_lo_{s}", [P, KD, P], F16) for s in "ABC"}
        gate = sb("gate", [P, 2, CH], F32)
        h = {s: sb(f"h_{s}", [P, H], F32) for s in "AC"}
        ht_hi = sb("ht_hi", [P, 2, 4, P], F16)
        ht_lo = sb("ht_lo", [P, 2, 4, P], F16)
        qk4 = sb("qk4", [P, HEADS, 4, DK], F16)
        qt = sb("qt", [P, 2, HEADS // 2, P], F16)
        kt = sb("kt", [P, HEADS // 2, BPS, P], F16)
        v = sb("v", [P, BPS, HEADS, 3, DK], BF16)
        prob = sb("prob", [P, 2, 4, 2 * P], F32)
        pt_hi = sb("pt_hi", [P, 8, P], F16)
        pt_lo = sb("pt_lo", [P, 8, P], F16)
        o_sum = sb("o_sum", [P, 8, DK], F32)
        o_norm = sb("o_norm", [P, D], F32)
        ot_hi = sb("ot_hi", [P, KD, P], F16)
        ot_lo = sb("ot_lo", [P, KD, P], F16)
        id32 = sb("id32", [P, P], F32)
        id16 = sb("id16", [P, P], F16)
        idb = sb("idb", [P, P], BF16)
        mask = sb("mask", [P, 2 * P], F32)
        zeros = sb("zeros", [P, P], F32)
        neg_half = sb("neg_half", [P, 1], F32)
        carrier = sb("carrier", [1, 384], F32)
        row_max = sb("row_max", [P, HEADS], F32)
        exp_bias = sb("exp_bias", [P, HEADS], F32)
        row_sum = sb("row_sum", [P, HEADS], F32)
        row_inv = sb("row_inv", [P, 8], F32)
        st6 = {s: sb(f"st6_{s}", [P, 6], F32) for s in "ABC"}
        mean_var = {s: sb(f"mean_var_{s}", [P, 2], F32) for s in "ABC"}
        var_eps = {s: sb(f"var_eps_{s}", [P, 1], F32) for s in "ABC"}
        rstd = {s: sb(f"rstd_{s}", [P, 1], F32) for s in "ABC"}
        sq_parts = {s: sb(f"sq_parts_{s}", [P, NC], F32) for s in "AC"}
        sq_sum = {s: sb(f"sq_sum_{s}", [P, 1], F32) for s in "AC"}
        sq_mean = {s: sb(f"sq_mean_{s}", [P, 1], F32) for s in "AC"}
        rms_inv = {s: sb(f"rms_inv_{s}", [P, 1], F32) for s in "AC"}
        w_absmax = sb("w_absmax", [P, 4], F32)
        w_max = sb("w_max", [P, 4], F32)
        w_floor = sb("w_floor", [P, 4], F32)
        w_pow2 = sb("w_pow2", [P, 4], F32)
        w_rec = sb("w_rec", [P, 4], F32)
        w_scale = sb("w_scale", [P, 4], F32)
        out_scale = sb("out_scale", [P, 1], F32)
        exp_scale = sb("exp_scale", [P, 1], F32)
        neg_exp_scale = sb("neg_exp_scale", [P, 1], F32)
        grp_sum = sb("grp_sum", [P, 2, G64], F32)
        grp_scale = sb("grp_scale", [P, 2, G64], BF16)
        kt_4k = [kt[:, 4 * n:4 * n + 4, :, :].rearrange("p a b c -> p (a b c)").bitcast(BF16) for n in range(4)]
        qt_4k = [qt[:, n, :, :].rearrange("p a b -> p (a b)").bitcast(BF16) for n in range(2)]
        prob_4k = [prob[:, n, :, :].rearrange("p a b -> p (a b)").bitcast(BF16) for n in range(2)]
        v_4k = [v[:, :, :, :, :].rearrange("p a b c d -> p (a b c d)")[:, 2048 * n:2048 * n + 2048] for n in range(2)]
        w_raw = [stream[:, 2:6, :].rearrange("p a b -> p (a b)"), h["C"][:, :]]
        w_abs = kt_4k[0:3]
        w_sign = [kt_4k[3], v_4k[1], qt_4k[0]]
        w_diff = [qk4[:, :, :, :].rearrange("p a b c -> p (a b c)").bitcast(BF16), qt_4k[1]]
        w_keep = v_4k[0]
        w_tern = prob_4k
        at_raw = [stream[:, 2:6, :], h["C"][:, :].rearrange("p (t d) -> p t d", t=4),
                  kt[:, 0:8, :, :].rearrange("p (t a) b c -> p t (a b c)", t=4).bitcast(F32),
                  prob[:, :, :, :].rearrange("p a (t b) c -> p (a t) (b c)", t=2)]
        ps_w = [(ps_s[:, 0:CH], ps_s[:, CH:2 * CH]), (ps_y[:, :], ps_o[:, :])]

        consts = sem("consts")
        ids = sem("ids")
        w_in = [sem(f"w_in{n}") for n in (0, 1)]
        w_mag = sem("w_mag")
        w_parts = sem("w_parts")
        w_sum = sem("w_sum")
        w_grp = sem("w_grp")
        w_dif = sem("w_dif")
        w_kp = sem("w_kp")
        w_step = sem("w_step")
        w_q = [sem(f"w_q{n}") for n in (0, 1)]
        w_tr = sem("w_tr")
        w_st = sem("w_st")
        a_in = [sem(f"a_in{m}") for m in range(4)]
        a_mx = sem("a_mx")
        a_all = sem("a_all")
        sc_step = sem("sc_step")
        a_tr = sem("a_tr")
        a_hi = sem("a_hi")
        a_lo = sem("a_lo")
        p_xt = {s: sem(f"p_xt_{s}") for s in "ABC"}
        p_up = {s: sem(f"p_up_{s}") for s in "AC"}
        p_ht = {s: sem(f"p_ht_{s}") for s in "AC"}
        p_dn = {s: sem(f"p_dn_{s}") for s in "AC"}
        p_q, p_k, p_v = sem("p_q"), sem("p_k"), sem("p_v")
        p_qt, p_kt = sem("p_qt"), sem("p_kt")
        p_s = sem("p_s")
        p_pt = sem("p_pt")
        p_pv = sem("p_pv")
        p_ot, p_wo = sem("p_ot"), sem("p_wo")
        a_xt = {s: sem(f"a_xt_{s}") for s in "ABC"}
        a_tanh = {s: sem(f"a_tanh_{s}") for s in "AC"}
        a_sq = {s: sem(f"a_sq_{s}") for s in "AC"}
        a_ht = {s: sem(f"a_ht_{s}") for s in "AC"}
        a_q, a_k, a_v = sem("a_q"), sem("a_k"), sem("a_v")
        a_kt = sem("a_kt")
        a_exp = sem("a_exp")
        a_pt = sem("a_pt")
        a_ot = sem("a_ot")
        d_xt = {s: sem(f"d_xt_{s}") for s in "ABC"}
        d_gate = {s: sem(f"d_gate_{s}") for s in "AC"}
        d_h = {s: sem(f"d_h_{s}") for s in "AC"}
        d_sqs = {s: sem(f"d_sqs_{s}") for s in "AC"}
        d_sqm = {s: sem(f"d_sqm_{s}") for s in "AC"}
        d_hn = {s: sem(f"d_hn_{s}") for s in "AC"}
        d_ht = {s: sem(f"d_ht_{s}") for s in "AC"}
        d_qlo, d_klo = sem("d_qlo"), sem("d_klo")
        d_q, d_k, d_v = sem("d_q"), sem("d_k"), sem("d_v")
        d_qt = sem("d_qt")
        d_mx = sem("d_mx")
        d_bias = sem("d_bias")
        d_pt = sem("d_pt")
        d_ot = sem("d_ot")
        d_osum, d_rinv = sem("d_osum"), sem("d_rinv")
        d_on = sem("d_on")
        d_x1, d_x2, d_x3 = sem("d_x1"), sem("d_x2"), sem("d_x3")
        d_st = {s: sem(f"d_st_{s}") for s in "ABC"}
        d_mv = {s: sem(f"d_mv_{s}") for s in "ABC"}
        d_ve = {s: sem(f"d_ve_{s}") for s in "ABC"}
        d_xh = {s: sem(f"d_xh_{s}") for s in "ABC"}
        g_rstd = {s: sem(f"g_rstd_{s}") for s in "ABC"}
        g_rms = {s: sem(f"g_rms_{s}") for s in "AC"}
        g_vm, g_v = sem("g_vm"), sem("g_v")
        x_in = [sem(f"x_in{n}") for n in (0, 1)]
        x_out = sem("x_out")

        NCONST = 7

        def need(eng, s, n):
            if not isinstance(n, int) or n > 0:
                eng.wait_ge(s, n)

        def last(b):
            return min(b, NB - 1) if isinstance(b, int) else b

        places = iter(range(384))

        def place_of_carrier():
            n = next(places)
            return carrier[0:1, n:n + 1]

        def on(b):
            return not isinstance(b, int) or 0 <= b < NB

        def slot(b):
            if isinstance(b, int):
                return stream[:, b % RING, :]
            return stream[:, bass.ds((b + RING) % RING, 1), :].rearrange("p a d -> p (a d)")

        STEADY, END = 5, NB + 4
        STEADY_END = STEADY + (NB - 1 - STEADY) // BPS * BPS

        def ternary_done(eng):
            eng.wait_ge(w_st, NTU)

        def early(i, hs):
            return isinstance(i, int) and i == 0 and hs < 4

        def early_chunk(n, behind):
            c = (n - 2 - behind) // 2
            return c if (n - 2 - behind) % 2 == 0 and 0 <= c < NC else None

        def half_of_weight(i, hs, behind):
            if not isinstance(i, int) or i not in (0, 1):
                return None
            n = hs - 6 - behind if i == 0 else hs + 2 - behind
            in_turn = (0 <= n < 2) if i == 0 else (2 - behind <= n < 8)
            return n if in_turn else None

        def all_iterations(eng, body, ternary_weights):
            body(-1, BPS - 1)
            ternary_weights()
            ternary_done(eng)
            for i in range(0, STEADY):
                body(i, i % BPS)
            with eng.Fori(0, (STEADY_END - STEADY) // BPS) as j:
                for n in range(BPS):
                    body(BPS * j + (STEADY + n), (STEADY + n) % BPS)
            for i in range(STEADY_END, END):
                body(i, i % BPS)

        def prob_t_view(tiles, place):
            if place:
                return tiles.rearrange("p a b -> p (a b)")
            return tiles.rearrange("p (j h) b -> p j h b", h=2)[:, :, 1, :]

        def spare(i, hs):
            if not isinstance(i, int):
                return None
            up_missing, down_missing = (not on(i), not on(i - 4)) if hs < 4 else (not on(i - 3), not on(i))
            return "gu" if up_missing else "ht_y" if down_missing else None

        def pt_banks(i, hs):
            return {None: (ps_s[:, 0:CH], ps_s[:, CH:2 * CH]), "gu": (ps_gu[:, 0:CH], ps_gu[:, CH:2 * CH]),
                    "ht_y": (ps_ht[:, :], ps_y[:, :])}[spare(i, hs)]

        def in_turn(s, b, n):
            return s == "C" and isinstance(b, int) and b == NB - 1 and n % 2 == 1

        def up_banks(s, b, c):
            return ps_s if in_turn(s, b, c) else ps_gu

        def hidden_bank(s, b, g):
            return ps_s[:, 0:CH] if in_turn(s, b, g) else ps_ht[:, :]

        def ps_t_view(bank, place):
            return bank if place else bank.rearrange("p (j h b) -> p j h b", h=2, b=P)[:, :, 1, :]

        block = ctx.enter_context(nc.Block())

        @block.sync
        def _(sp):
            def ternary_weights():
                for n, u in enumerate(UNITS):
                    if n == 2:
                        load_x(1, 1)
                    need(sp, w_parts, n - 1)
                    if u < NGU:
                        sp.dma_start(w_raw[n % 2].rearrange("p (t d) -> p t d", t=4),
                                     gu_units[u]).then_inc(w_in[n % 2], 16)
                    else:
                        sp.dma_start(w_raw[n % 2], wp_units[u - NGU]).then_inc(w_in[n % 2], 16)
                sp.wait_ge(w_parts, NTU)
                sp.dma_start(at_raw[Q], at_units[Q]).then_inc(a_in[Q], 16)
                sp.dma_start(at_raw[K], at_units[K]).then_inc(a_in[K], 16)
                for n in (0, 1):
                    sp.wait_ge(w_q[n], NTU // 2)
                sp.dma_start(at_raw[V], at_units[V]).then_inc(a_in[V], 16)
                sp.wait_ge(w_tr, NTU)
                sp.dma_start(at_raw[O], at_units[O]).then_inc(a_in[O], 16)

            def load_x(b, place):
                rows = slice(b * P, (b + 1) * P) if isinstance(b, int) else bass.ds(b * P, P)
                sp.dma_start(slot(b), xf[rows, :]).then_inc(x_in[place % 2], 16)

            def body(i, place):
                b = i + 1
                if on(b) and not (isinstance(b, int) and b == 1):
                    need(sp, x_out, 16 * (b - 5))
                    if isinstance(b, int) and b == 2:
                        sp.wait_ge(a_tr, 2)
                    if isinstance(b, int):
                        need(sp, x_in[b % 2], 16 * (b // 2))
                    load_x(b, place + 1)
                b = i - 4
                if on(b):
                    sp.wait_ge(d_x3, b + 1)
                    rows = slice(b * P, (b + 1) * P) if isinstance(b, int) else bass.ds(b * P, P)
                    sp.dma_start(of[rows, :], slot(b)).then_inc(x_out, 16)

            all_iterations(sp, body, ternary_weights)
            sp.wait_ge(x_out, 16 * NB)

        @block.gpsimd
        def _(pool):
            pool.memset(id32[:, :], 0.0).then_inc(consts, 1)
            pool.memset(mask[:, :], 0.0).then_inc(consts, 1)
            pool.memset(zeros[:, :], 0.0).then_inc(consts, 1)
            pool.memset(neg_half[:, :], -0.5).then_inc(consts, 1)
            pool.wait_ge(consts, 4)
            pool.affine_select(out=id32[:, :], in_=id32[:, :], compare_op=ALU.not_equal, fill=1.0, base=0,
                               pattern=[[-1, P]], channel_multiplier=1).then_inc(consts, 1)
            pool.affine_select(out=mask[:, 0:P], in_=mask[:, 0:P], compare_op=ALU.is_ge, fill=NEG, base=0,
                               pattern=[[1, P]], channel_multiplier=-1).then_inc(consts, 1)
            pool.affine_select(out=mask[:, P:2 * P], in_=mask[:, P:2 * P], compare_op=ALU.is_ge, fill=NEG, base=0,
                               pattern=[[-1, P]], channel_multiplier=1).then_inc(consts, 1)

            def ternary_weights():
                def differ(n):
                    pool.wait_ge(w_grp, n + 1)
                    need(pool, w_q[n % 2], n // 2)
                    pool.tensor_tensor(out=w_diff[n % 2].rearrange("p (g k) -> p g k", g=G64),
                                       in0=grp_scale[:, n % 2, :].unsqueeze(2).to_broadcast([P, G64, 64]),
                                       in1=w_abs[n % 3].rearrange("p (g k) -> p g k", g=G64),
                                       op=ALU.subtract).then_inc(w_dif, 1)

                def give_sign(n):
                    pool.wait_ge(w_step, 2 * n + 2)
                    pool.wait_ge(w_parts, n + 1)
                    need(pool, w_tr, n - 1)
                    pool.tensor_tensor(out=w_tern[n % 2], in0=w_diff[n % 2], in1=w_sign[n % 3],
                                       op=ALU.mult).then_inc(w_q[1], 1)

                for n in range(NTU):
                    differ(n)
                    if n % 2 == 0 and n > 0:
                        give_sign(n - 1)
                power("A", rms_inv["A"], sq_mean["A"], d_sqm["A"], g_rms["A"], 0)

            pool.wait_ge(consts, NCONST)

            def power(s, dst, src, ready, done, b):
                pool.wait_ge(ready, b + 1)
                pool.tensor_tensor(out=dst[:, :], in0=src[:, :], in1=neg_half[:, :], op=ALU.pow).then_inc(done, 1)

            def body(i, place):
                if on(i - 1):
                    power("B", rstd["B"], var_eps["B"], d_ve["B"], g_rstd["B"], i - 1)
                if on(i - 3):
                    power("C", rstd["C"], var_eps["C"], d_ve["C"], g_rstd["C"], i - 3)
                if on(i) and not early(i, 3):
                    power("A", rms_inv["A"], sq_mean["A"], d_sqm["A"], g_rms["A"], i)
                if on(i + 1):
                    power("A", rstd["A"], var_eps["A"], d_ve["A"], g_rstd["A"], i + 1)
                if on(i - 3):
                    power("C", rms_inv["C"], sq_mean["C"], d_sqm["C"], g_rms["C"], i - 3)
                if on(i - 1):
                    b = i - 1
                    pool.wait_ge(d_v, b + 1)
                    vr = v_rest[:, :].rearrange("p (h d) -> p h d", d=DK)
                    mine = v[:, (place - 1) % BPS, :, :, :]
                    pool.tensor_tensor(out=mine[:, :, 1, :], in0=vr,
                                       in1=zeros[:, 0:1].unsqueeze(2).to_broadcast([P, HEADS, DK]),
                                       op=ALU.add).then_inc(g_vm, 1)
                    pool.wait_ge(g_vm, b + 1)
                    pool.tensor_tensor(out=mine[:, :, 2, :], in0=vr, in1=mine[:, :, 1, :],
                                       op=ALU.subtract).then_inc(g_v, 1)
                if isinstance(i, int) and i == 0:
                    pool.wait_ge(a_mx, 4)
                    pool.partition_all_reduce(w_max[:, :], w_absmax[:, :], P, RMAX).then_inc(a_all, 1)

            all_iterations(pool, body, ternary_weights)

        @block.scalar
        def _(act):
            def ternary_weights():
                def parts(n):
                    act.wait_ge(w_in[n % 2], 16 * (n // 2 + 1))
                    need(act, w_q[(n - 3) % 2], (n - 3) // 2 + 1)
                    act.activation(w_abs[n % 3], w_raw[n % 2], ACT.Abs).then_inc(w_mag, 1)
                    act.activation(w_sign[n % 3], w_raw[n % 2], ACT.Sign).then_inc(w_parts, 1)

                def store(n):
                    u = UNITS[n]
                    act.wait_ge(w_tr, n + 1)
                    dst = (wgu_t[:, :, u * 512:(u + 1) * 512] if u < NGU else
                           wp_t[:, :, (u - NGU) * P:(u - NGU + 1) * P])
                    k = dst.shape[1] // 2
                    for half in (0, 1):
                        s = act.activation(dst[:, k * half:k * half + k, :],
                                           ps_w[n % 2][half].bitcast(BF16).rearrange("p (a b) -> p a b", a=k), ACT.Copy)
                    s.then_inc(w_st, 1)

                for n in range(NTU + 3):
                    if n < NTU:
                        parts(n)
                    if n >= 3:
                        store(n - 3)
                    if early_chunk(n - 3, 0) is not None:
                        c = early_chunk(n - 3, 0)
                        half_tanh("A", 0, c, c % 2)
                    if early_chunk(n - 3, 2) is not None:
                        c = early_chunk(n - 3, 2)
                        square("A", 0, c, c % 2)

            def attention_weight(n):
                m, k = n // 2, slice(n % 2 * 2, n % 2 * 2 + 2)
                act.wait_ge(a_tr, n + 1)
                act.wait_ge(sc_step, 7)
                act.activation(wat_hi[m][:, k, :], ps_s[:, :].rearrange("p (k d) -> p k d", k=2), ACT.Copy,
                               scale=w_scale[:, m:m + 1]).then_inc(a_hi, 1)

            def copy_hi(dst, src, ready, n, done, scale=1.0):
                act.wait_ge(ready, n)
                act.activation(dst, src, ACT.Copy, scale=scale).then_inc(done, 1)

            def xt_piece(s, b):
                copy_hi(xt_hi[s][:, :, :].rearrange("p a b -> p (a b)"), ps_m[:, :], p_xt[s], b + 1, a_xt[s])

            def half_tanh(s, b, c, n):
                act.wait_ge(p_up[s], 8 * b + 2 * c + 1)
                act.activation(gate[:, n, :], up_banks(s, b, c)[:, 0:CH], ACT.Tanh, scale=0.5 * 2.0 ** -XS_LOG2)\
                   .then_inc(a_tanh[s], 1)

            def square(s, b, c, n):
                act.wait_ge(d_h[s], 4 * b + c + 1)
                act.activation(gate[:, n, :], h[s][:, c * CH:(c + 1) * CH], ACT.Square,
                               accum_out=sq_parts[s][:, c:c + 1]).then_inc(a_sq[s], 1)

            def exps(b, q, place):
                act.wait_ge(d_bias, 8 * b + q + 1)
                keys = slice(0 if place else P, 2 * P)
                for j in range(4):
                    hd = 4 * q + j
                    p = prob[:, q % 2, j, keys]
                    e = act.activation(p, p, ACT.Exp, bias=exp_bias[:, hd:hd + 1], scale=exp_scale[:, 0:1],
                                       accum_out=row_sum[:, hd:hd + 1])
                e.then_inc(a_exp, 1)

            def prob_hi(b, q, banks, place):
                for pair in range(2):
                    copy_hi(prob_t_view(pt_hi[:, 4 * pair:4 * pair + 4, :], place), ps_t_view(banks[pair], place),
                            p_pt, 16 * b + 2 * q + pair + 1, a_pt)

            def head_view(ap):
                return ap.rearrange("p (h d) -> p h d", d=DK)

            def body(i, place):
                bL, bA, bQ, bT, bW, bE = i + 1, i, i - 1, i - 2, i - 3, i - 4
                for hs in range(8):
                    up, bu = ("A", bA) if hs < 4 else ("C", bW)
                    dn, bd = ("C", bE) if hs < 4 else ("A", bA)
                    c = hs % 4
                    bp, qp, p_place = (bW, 7, place - 3) if hs < 1 else (bT, hs - 1, place - 2)
                    p_place %= BPS
                    if half_of_weight(i, hs, 1) is not None:
                        attention_weight(half_of_weight(i, hs, 1))
                    if on(bp):
                        exps(bp, qp, p_place)
                    if hs == 1 and on(bQ):
                        act.wait_ge(p_q, bQ + 1)
                        act.activation(qk4[:, :, 0, :], head_view(ps_m[:, :]), ACT.Copy,
                                       scale=2.0 ** -DOWN_LOG2).then_inc(a_q, 1)
                    if hs == 4 and on(bQ):
                        act.wait_ge(p_k, bQ + 1)
                        act.activation(qk4[:, :, 0, :], head_view(ps_m[:, :]), ACT.Copy,
                                       scale=2.0 ** -DOWN_LOG2).then_inc(a_k, 1)
                    if on(bu) and not early(i, hs):
                        half_tanh(up, bu, c, hs % 2)
                    if on(bd):
                        copy_hi(ht_hi[:, c % 2, :, :].rearrange("p a b -> p (a b)"), hidden_bank(dn, bd, c),
                                p_ht[dn], 4 * bd + c + 1, a_ht[dn])
                    if hs == 0 and on(bQ):
                        xt_piece("B", bQ)
                    if hs == 2 and on(bW):
                        copy_hi(ot_hi[:, :, :].rearrange("p a b -> p (a b)"), ps_m[:, :], p_ot, bW + 1, a_ot)
                    if hs == 3 and on(bW):
                        xt_piece("C", bW)
                    if on(bp):
                        prob_hi(bp, qp, pt_banks(i, hs), p_place)
                    if hs == 4 and on(bQ):
                        copy_hi(kt[:, 0:8, (place - 1) % BPS, :], ps_m16, p_kt, 2 * bQ + 1, a_kt)
                    if hs == 5 and on(bQ):
                        copy_hi(kt[:, 8:16, (place - 1) % BPS, :], ps_m16, p_kt, 2 * bQ + 2, a_kt)
                    if hs == 6 and on(bL):
                        xt_piece("A", bL)
                    if on(bu) and not early(i, hs):
                        square(up, bu, c, hs % 2)
                    if hs == 7 and on(bQ):
                        act.wait_ge(p_v, bQ + 1)
                        act.activation(v[:, (place - 1) % BPS, :, 0, :], head_view(ps_m[:, :]), ACT.Copy,
                                       scale=2.0 ** -DOWN_LOG2).then_inc(a_v, 1)

            all_iterations(act, body, ternary_weights)

        @block.vector
        def _(dve):
            def hold():
                dve.memset(place_of_carrier(), 0.0)

            dve.wait_ge(consts, NCONST)
            dve.tensor_copy(id16[:, :], id32[:, :]).then_inc(ids, 1)
            dve.tensor_copy(idb[:, :], id32[:, :]).then_inc(ids, 1)

            def ternary_weights():
                def scales(n):
                    dve.wait_ge(w_mag, n + 1)
                    dve.tensor_reduce(grp_sum[:, n % 2, :], w_abs[n % 3].rearrange("p (g k) -> p g k", g=G64), AX.X,
                                      ALU.add).then_inc(w_sum, 1)
                    dve.wait_ge(w_sum, n + 1)
                    need(dve, w_dif, n - 1)
                    dve.tensor_scalar(grp_scale[:, n % 2, :], grp_sum[:, n % 2, :], 1.0 / 64, CLIP_MIN,
                                      ALU.mult, ALU.max).then_inc(w_grp, 1)

                def quantise(n):
                    diff, w = w_diff[n % 2], w_abs[n % 3]
                    dve.wait_ge(w_dif, n + 1)
                    dve.tensor_tensor(out=w_keep, in0=w, in1=diff, op=ALU.is_gt).then_inc(w_kp, 1)
                    dve.wait_ge(w_kp, n + 1)
                    dve.tensor_tensor(out=diff, in0=w, in1=diff, op=ALU.add).then_inc(w_step, 1)
                    dve.wait_ge(w_step, 2 * n + 1)
                    dve.tensor_tensor(out=diff, in0=diff, in1=w_keep, op=ALU.mult).then_inc(w_step, 1)
                    if n % 2 == 0 or n == NTU - 1:
                        dve.wait_ge(w_step, 2 * n + 2)
                        dve.wait_ge(w_parts, n + 1)
                        need(dve, w_tr, n - 1)
                        dve.tensor_tensor(out=w_tern[n % 2], in0=diff, in1=w_sign[n % 3],
                                          op=ALU.mult).then_inc(w_q[n % 2], 1)

                for n in range(NTU + 1):
                    if n < NTU:
                        scales(n)
                    if n > 0:
                        quantise(n - 1)
                    if early_chunk(n - 1, 2) is not None:
                        c = early_chunk(n - 1, 2)
                        gated("A", 0, c, c % 2)
                        hidden("A", 0, c, c % 2)
                rms_stats("A", 0)
                rms_apply("A", 0, False)
                rms_apply("A", 0, True)
                largest(Q)
                largest(K)

            def largest(m):
                dve.wait_ge(a_in[m], 16)
                dve.tensor_reduce(w_absmax[:, m:m + 1], at_raw[m], AX.XY, ALU.max,
                                  apply_absolute_value=True).then_inc(a_mx, 1)

            def attention_scales():
                dve.wait_ge(a_all, 1)
                dve.tensor_scalar(w_floor[:, :], w_max[:, :], 2.0 ** -40, None, ALU.max).then_inc(sc_step, 1)
                dve.wait_ge(sc_step, 1)
                dve.tensor_scalar(w_pow2[:, :].bitcast(U32), w_floor[:, :].bitcast(U32), 0x7F800000, None,
                                  ALU.bitwise_and).then_inc(sc_step, 1)
                dve.wait_ge(sc_step, 2)
                dve.reciprocal(w_rec[:, :], w_pow2[:, :]).then_inc(sc_step, 1)
                dve.wait_ge(sc_step, 3)
                dve.tensor_scalar(w_scale[:, :], w_rec[:, :], 2.0 ** WS_LOG2, None, ALU.mult).then_inc(sc_step, 1)
                dve.tensor_scalar(exp_scale[:, :], w_pow2[:, Q:Q + 1], w_pow2[:, K:K + 1],
                                  2.0 ** -10 / math.sqrt(DK), ALU.mult, ALU.mult).then_inc(sc_step, 1)
                dve.tensor_scalar(out_scale[:, :], w_pow2[:, V:V + 1], w_pow2[:, O:O + 1],
                                  2.0 ** -(5 + WS_LOG2), ALU.mult, ALU.mult).then_inc(sc_step, 1)
                dve.wait_ge(sc_step, 6)
                dve.tensor_scalar(neg_exp_scale[:, :], exp_scale[:, :], -1.0, None, ALU.mult).then_inc(sc_step, 1)
                dve.wait_ge(sc_step, 7)

            def attention_weight(n):
                m, k = n // 2, slice(n % 2 * 2, n % 2 * 2 + 2)
                dve.wait_ge(a_hi, n + 1)
                dve.scalar_tensor_tensor(out=wat_lo[m][:, k, :], in0=ps_s[:, :].rearrange("p (k d) -> p k d", k=2),
                                         scalar=w_scale[:, m:m + 1], in1=wat_hi[m][:, k, :], op0=ALU.mult,
                                         op1=ALU.subtract).then_inc(a_lo, 1)

            def flat(ap):
                return ap.rearrange("p a b -> p (a b)")

            def head_view(ap):
                return ap.rearrange("p (h d) -> p h d", d=DK)

            def norm_stats(s, b, ready, n, scale):
                dve.wait_ge(ready, n)
                hold()
                dve.bn_stats(st6[s][:, :], slot(b)).then_inc(d_st[s], 1)
                dve.wait_ge(d_st[s], b + 1)
                hold()
                dve.bn_aggr(mean_var[s][:, :], st6[s][:, :]).then_inc(d_mv[s], 1)
                dve.wait_ge(d_mv[s], b + 1)
                dve.tensor_scalar(var_eps[s][:, :], mean_var[s][:, 1:2], LN_EPS, scale, ALU.add, ALU.mult)\
                   .then_inc(d_ve[s], 1)

            def norm_apply(s, b):
                dve.wait_ge(g_rstd[s], b + 1)
                dve.tensor_scalar(xhat[:, :], slot(b), mean_var[s][:, 0:1], rstd[s][:, 0:1],
                                  ALU.subtract, ALU.mult).then_inc(d_xh[s], 1)

            def rms_stats(s, b):
                dve.wait_ge(a_sq[s], 4 * b + 4)
                dve.tensor_reduce(sq_sum[s][:, :], sq_parts[s][:, :], AX.X, ALU.add).then_inc(d_sqs[s], 1)
                dve.wait_ge(d_sqs[s], b + 1)
                down = 2.0 ** (-2 * HS_LOG2)
                dve.tensor_scalar(sq_mean[s][:, :], sq_sum[s][:, :], down / H, down * RMS_EPS,
                                  ALU.mult, ALU.add).then_inc(d_sqm[s], 1)

            def rms_apply(s, b, rest):
                at = slice(CH, H) if rest else slice(0, CH)
                dve.wait_ge(g_rms[s], b + 1)
                dve.tensor_scalar(h[s][:, at], h[s][:, at], rms_inv[s][:, 0:1], None, ALU.mult).then_inc(d_hn[s], 1)

            def masked_max(b, q, place):
                dve.wait_ge(p_s, 8 * b + q + 1)
                hold()
                first = 0 if place else P
                for pair in range(2):
                    for o in range(2):
                        hd = 4 * q + 2 * pair + o
                        at = o * CH + pair * 2 * P
                        m = dve.tensor_tensor_reduce(prob[:, q % 2, 2 * pair + o, first:2 * P],
                                                     ps_s[:, at + first:at + 2 * P], mask[:, first:2 * P],
                                                     1.0, NEG, ALU.add, ALU.max, row_max[:, hd:hd + 1])
                m.then_inc(d_mx, 1)
                dve.wait_ge(d_mx, 8 * b + q + 1)
                dve.tensor_scalar(exp_bias[:, 4 * q:4 * q + 4], row_max[:, 4 * q:4 * q + 4], neg_exp_scale[:, 0:1],
                                  PROB_LOG2 * math.log(2.0), ALU.mult, ALU.add).then_inc(d_bias, 1)

            def gated(s, b, c, n):
                dve.wait_ge(a_tanh[s], 4 * b + c + 1)
                dve.scalar_tensor_tensor(out=gate[:, n, :], in0=gate[:, n, :], scalar=1.0,
                                         in1=up_banks(s, b, c)[:, 0:CH], op0=ALU.add, op1=ALU.mult).then_inc(d_gate[s], 1)

            def hidden(s, b, c, n):
                dve.wait_ge(d_gate[s], 4 * b + c + 1)
                dve.wait_ge(p_up[s], 8 * b + 2 * c + 2)
                dve.scalar_tensor_tensor(out=h[s][:, c * CH:(c + 1) * CH], in0=up_banks(s, b, c)[:, CH:2 * CH],
                                         scalar=0.5 * 2.0 ** (-2 * XS_LOG2), in1=gate[:, n, :], op0=ALU.mult,
                                         op1=ALU.mult).then_inc(d_h[s], 1)

            def take_lo(dst, src, hi, ready, n, done):
                dve.wait_ge(ready, n)
                dve.tensor_tensor(out=dst, in0=src, in1=hi, op=ALU.subtract).then_inc(done, 1)

            def prob_lo(b, q, banks, place):
                for pair in range(2):
                    tiles = slice(4 * pair, 4 * pair + 4)
                    take_lo(prob_t_view(pt_lo[:, tiles, :], place), ps_t_view(banks[pair], place),
                            prob_t_view(pt_hi[:, tiles, :], place), a_pt, 16 * b + 2 * q + pair + 1, d_pt)

            def normalise_o(b, ct):
                dve.wait_ge(p_pv, 8 * b + 2 * ct + 2)
                o = ps_o[:, 0:8 * 3 * DK].rearrange("p (h t d) -> p h d t", h=8, t=3)
                dve.tensor_reduce(o_sum[:, :, :], o, AX.X, ALU.add).then_inc(d_osum, 1)
                dve.reciprocal(row_inv[:, :], row_sum[:, 8 * ct:8 * ct + 8]).then_inc(d_rinv, 1)
                dve.wait_ge(d_osum, 4 * b + ct + 1)
                dve.wait_ge(d_rinv, 4 * b + ct + 1)
                dve.tensor_tensor(out=head_view(o_norm[:, ct * P:(ct + 1) * P]), in0=o_sum[:, :, :],
                                  in1=row_inv[:, :].unsqueeze(2).to_broadcast([P, 8, DK]),
                                  op=ALU.mult).then_inc(d_on, 1)

            def add_ffn(s, b, done):
                dve.wait_ge(p_dn[s], 4 * b + 4)
                dve.scalar_tensor_tensor(out=slot(b), in0=ps_y[:, :], scalar=0.5 * 2.0 ** -HS_LOG2, in1=slot(b),
                                         op0=ALU.mult, op1=ALU.add).then_inc(done, 1)

            def body(i, place):
                bL, bA, bQ, bT, bW, bE = i + 1, i, i - 1, i - 2, i - 3, i - 4
                for hs in range(8):
                    up, bu = ("A", bA) if hs < 4 else ("C", bW)
                    dn, bd = ("C", bE) if hs < 4 else ("A", bA)
                    c = hs % 4
                    bp, qp, p_place = (bW, 7, place - 3) if hs < 1 else (bT, hs - 1, place - 2)
                    p_place %= BPS
                    bv, qv, v_place = (bW, hs + 6, place - 3) if hs < 2 else (bT, hs - 2, place - 2)
                    v_place %= BPS
                    if isinstance(i, int) and i == 0:
                        if hs in (5, 6):
                            largest({5: V, 6: O}[hs])
                        elif hs == 7:
                            attention_scales()
                    if half_of_weight(i, hs, 1) is not None:
                        attention_weight(half_of_weight(i, hs, 1))
                    if hs == 0 and on(bQ):
                        norm_stats("B", bQ, d_x1, bQ + 1, 2.0 ** (-2 * XS_LOG2))
                    if hs == 1 and on(bL):
                        odd = (place + 1) % 2
                        norm_stats("A", bL, x_in[odd], 8 * (bL - odd) + 16, 2.0 ** (-2 * XS_LOG2))
                    if hs == 1 and on(bQ):
                        dve.wait_ge(a_q, bQ + 1)
                        dve.scalar_tensor_tensor(out=qk4[:, :, 1, :], in0=head_view(ps_m[:, :]),
                                                 scalar=2.0 ** -DOWN_LOG2, in1=qk4[:, :, 0, :], op0=ALU.mult,
                                                 op1=ALU.subtract).then_inc(d_qlo, 1)
                        dve.wait_ge(d_qlo, bQ + 1)
                        dve.tensor_copy(qk4[:, :, 2:4, :], qk4[:, :, 0:2, :]).then_inc(d_q, 1)
                    if hs == 3 and on(bW):
                        dve.wait_ge(p_wo, bW + 1)
                        dve.scalar_tensor_tensor(out=slot(bW), in0=ps_m[:, :], scalar=out_scale[:, 0:1],
                                                 in1=slot(bW), op0=ALU.mult, op1=ALU.add).then_inc(d_x2, 1)
                        norm_stats("C", bW, d_x2, bW + 1, 2.0 ** (-2 * XS_LOG2))
                    if hs == 4 and on(bQ):
                        k4 = qk4[:, :, :, :].rearrange("p h (a b) d -> p h a b d", b=2)
                        dve.wait_ge(a_k, bQ + 1)
                        dve.scalar_tensor_tensor(out=qk4[:, :, 2, :], in0=head_view(ps_m[:, :]),
                                                 scalar=2.0 ** -DOWN_LOG2, in1=qk4[:, :, 0, :], op0=ALU.mult,
                                                 op1=ALU.subtract).then_inc(d_klo, 1)
                        dve.wait_ge(d_klo, bQ + 1)
                        dve.tensor_copy(k4[:, :, :, 1, :], k4[:, :, :, 0, :]).then_inc(d_k, 1)
                    if on(bT):
                        masked_max(bT, hs, (place - 2) % BPS)
                    if hs == 2 and on(bQ):
                        dve.wait_ge(p_qt, 2 * bQ + 2)
                        dve.tensor_copy(qt[:, (place - 1) % 2, 8:16, :], ps_m16).then_inc(d_qt, 1)
                    if hs == 0 and on(bQ):
                        need(dve, p_xt["A"], last(i) + 1)
                        norm_apply("B", bQ)
                    if hs == 3 and on(bW):
                        if on(bQ):
                            dve.wait_ge(p_xt["B"], bQ + 1)
                        else:
                            dve.wait_ge(p_xt["C"], bW)
                        norm_apply("C", bW)
                    if on(bu) and not early(i, hs):
                        gated(up, bu, c, hs % 2)
                        if hs not in (0, 3):
                            hidden(up, bu, c, hs % 2)
                    if on(bd):
                        take_lo(flat(ht_lo[:, c % 2, :, :]), hidden_bank(dn, bd, c), flat(ht_hi[:, c % 2, :, :]),
                                a_ht[dn], 4 * bd + c + 1, d_ht[dn])
                    if on(bu) and hs in (0, 3) and not early(i, hs):
                        hidden(up, bu, c, hs % 2)
                    if hs == 0 and on(bQ):
                        take_lo(flat(xt_lo["B"][:, :, :]), ps_m[:, :], flat(xt_hi["B"][:, :, :]),
                                a_xt["B"], bQ + 1, d_xt["B"])
                    if hs == 2 and on(bW):
                        take_lo(flat(ot_lo[:, :, :]), ps_m[:, :], flat(ot_hi[:, :, :]), a_ot, bW + 1, d_ot)
                    if hs == 3 and on(bW):
                        take_lo(flat(xt_lo["C"][:, :, :]), ps_m[:, :], flat(xt_hi["C"][:, :, :]),
                                a_xt["C"], bW + 1, d_xt["C"])
                    if on(bp):
                        prob_lo(bp, qp, pt_banks(i, hs), p_place)
                    if hs == 1 and on(bQ):
                        dve.wait_ge(p_qt, 2 * bQ + 1)
                        dve.tensor_copy(qt[:, (place - 1) % 2, 0:8, :], ps_m16).then_inc(d_qt, 1)
                    if hs == 6 and on(bL):
                        take_lo(flat(xt_lo["A"][:, :, :]), ps_m[:, :], flat(xt_hi["A"][:, :, :]),
                                a_xt["A"], bL + 1, d_xt["A"])
                    if hs == 3 and on(bA) and not early(i, hs):
                        rms_stats("A", bA)
                    if hs == 7 and on(bW):
                        rms_stats("C", bW)
                    if hs % 2 and on(bv):
                        normalise_o(bv, qv // 2)
                    if hs == 3 and on(bE):
                        add_ffn("C", bE, d_x3)
                    if hs == 3 and on(bA) and not early(i, hs):
                        rms_apply("A", bA, False)
                    if hs == 4 and on(bA) and not early(i, 3):
                        rms_apply("A", bA, True)
                    if hs == 5 and on(bL):
                        if on(bW):
                            dve.wait_ge(p_xt["C"], bW + 1)
                        elif on(bQ):
                            dve.wait_ge(p_xt["B"], bQ + 1)
                        else:
                            need(dve, p_xt["A"], bL)
                        norm_apply("A", bL)
                    if hs == 7 and on(bA):
                        add_ffn("A", bA, d_x1)
                    if hs == 7 and on(bW):
                        rms_apply("C", bW, False)
                        if isinstance(i, int) and bW == NB - 1:
                            rms_apply("C", bW, True)
                    if hs == 7 and on(bQ):
                        dve.wait_ge(a_v, bQ + 1)
                        need(dve, g_v, bQ)
                        dve.scalar_tensor_tensor(out=head_view(v_rest[:, :]), in0=head_view(ps_m[:, :]),
                                                 scalar=2.0 ** -DOWN_LOG2, in1=v[:, (place - 1) % BPS, :, 0, :],
                                                 op0=ALU.mult, op1=ALU.subtract).then_inc(d_v, 1)
                    if hs == 0 and on(bE) and not (isinstance(i, int) and bE == NB - 1):
                        rms_apply("C", bE, True)

            all_iterations(dve, body, ternary_weights)

        @block.tensor
        def _(pe):
            pe.wait_ge(ids, 2)

            def ternary_weights():
                for n, u in enumerate(UNITS):
                    if early_chunk(n, 1) is not None:
                        c = early_chunk(n, 1)
                        pe.wait_ge(w_st, 2 * c + 2)
                        need(pe, d_h["A"], c)
                        if c == 0:
                            pe.wait_ge(d_xt["A"], 1)
                        up("A", 0, c)
                    pe.wait_ge(w_q[n % 2], n // 2 + 1)
                    need(pe, w_st, n - 1)
                    for a in range(4):
                        for k in range(4):
                            src = (4 * a + k) * P
                            tile = 4 * k + a if u < NGU else 4 * a + k
                            bank = ps_w[n % 2][tile // 8].bitcast(BF16)
                            t = pe.transpose(bank[:, tile % 8 * P:tile % 8 * P + P], w_tern[n % 2][:, src:src + P],
                                             idb[:, :])
                    t.then_inc(w_tr, 1)

            def attention_weight(n):
                m = n // 2
                pe.wait_ge(a_in[m], 16)
                need(pe, a_hi, n)
                need(pe, a_lo, n)
                for k in range(2):
                    for a in range(4):
                        row = (n % 2 * 2 + k) * P
                        t = pe.transpose(ps_s[:, k * CH + a * P:k * CH + (a + 1) * P], at_raw[m][:, a, row:row + P],
                                         id32[:, :])
                t.then_inc(a_tr, 1)

            def xt_piece(s, b):
                pe.wait_ge(d_xh[s], b + 1)
                for k in range(KD):
                    t = pe.transpose(ps_m[:, k * P:(k + 1) * P], xhat[:, k * P:(k + 1) * P], id32[:, :])
                t.then_inc(p_xt[s], 1)

            def up(s, b, c):
                for half in (0, 1):
                    n = 0
                    for k in range(KD):
                        for part in (xt_hi[s], xt_lo[s]):
                            t = pe.matmul(up_banks(s, b, c)[:, half * CH:(half + 1) * CH], part[:, k, :],
                                          wgu_t[:, k, half * H + c * CH:half * H + (c + 1) * CH],
                                          start=(n == 0), stop=(n == 2 * KD - 1))
                            n += 1
                    t.then_inc(p_up[s], 1)

            def hidden_t(s, b, g):
                for j in range(4):
                    at = (4 * g + j) * P
                    t = pe.transpose(hidden_bank(s, b, g)[:, j * P:(j + 1) * P], h[s][:, at:at + P], id32[:, :])
                t.then_inc(p_ht[s], 1)

            def down(s, b, g):
                for part, ready in ((ht_hi, a_ht[s]), (ht_lo, d_ht[s])):
                    pe.wait_ge(ready, 4 * b + g + 1)
                    for j in range(4):
                        t = pe.matmul(ps_y[:, :], part[:, g % 2, j, :], wp_t[:, 4 * g + j, :],
                                      start=(g == 0 and j == 0 and part is ht_hi),
                                      stop=(g == 3 and j == 3 and part is ht_lo))
                t.then_inc(p_dn[s], 1)

            def project(m, hi, lo, done, ks=range(KD)):
                for k in ks:
                    for n, (part, w) in enumerate(((hi, wat_hi), (hi, wat_lo), (lo, wat_hi))):
                        t = pe.matmul(ps_m[:, :], part[:, k, :], w[m][:, k, :], start=(k == 0 and n == 0),
                                      stop=(k == KD - 1 and n == 2))
                if ks[-1] == KD - 1:
                    t.then_inc(done, 1)

            def heads_t(f, done):
                for j in range(8):
                    pair = 8 * f + j
                    t = pe.transpose(ps_m16[:, j, :],
                                     qk4[:, 2 * pair:2 * pair + 2, :, :].rearrange("p a b c -> p (a b c)"), id16[:, :])
                t.then_inc(done, 1)

            def scores(b, q, place):
                for pair in range(2):
                    for o in range(2):
                        at = o * CH + pair * 2 * P
                        rows = slice(64 * o, 64 * o + 64)
                        if place:
                            out_at, keys = slice(at, at + 2 * P), slice(place - 1, place + 1)
                        else:
                            out_at, keys = slice(at + P, at + 2 * P), slice(0, 1)
                        t = pe.matmul(ps_s[:, out_at], qt[rows, place % 2, 2 * q + pair, :],
                                      kt[rows, 2 * q + pair, keys, :].rearrange("p a b -> p (a b)"),
                                      start=True, stop=True)
                t.then_inc(p_s, 1)

            def prob_t(b, q, banks, place):
                pe.wait_ge(a_exp, 8 * b + q + 1)
                for pair in range(2):
                    for j in (2 * pair, 2 * pair + 1):
                        for half in ((0, 1) if place else (1,)):
                            at = (2 * j + half) % 4 * P
                            t = pe.transpose(banks[pair][:, at:at + P], prob[:, q % 2, j, half * P:(half + 1) * P],
                                             id32[:, :])
                    t.then_inc(p_pt, 1)

            def prob_v(b, q, place):
                pe.wait_ge(d_pt, 16 * b + 2 * q + 2)
                for j in range(4):
                    hd = 4 * q + j
                    at = (hd % 8) * 3 * DK
                    products = [(half, part) for half in ((0, 1) if place else (1,)) for part in (pt_hi, pt_lo)]
                    for n, (half, part) in enumerate(products):
                        t = pe.matmul(ps_o[:, at:at + 3 * DK], part[:, 2 * j + half, :],
                                      v[:, place - 1 + half, hd, :, :].rearrange("p a b -> p (a b)"),
                                      start=(n == 0), stop=(n == len(products) - 1))
                t.then_inc(p_pv, 1)

            def body(i, place):
                bL, bA, bQ, bT, bW, bE = i + 1, i, i - 1, i - 2, i - 3, i - 4

                def first_use(m):
                    if isinstance(i, int) and i == 1:
                        pe.wait_ge(a_hi, 2 * m + 2)
                        pe.wait_ge(a_lo, 2 * m + 2)

                for hs in range(8):
                    c = hs % 4
                    bp, qp, p_place = (bW, 7, place - 3) if hs < 1 else (bT, hs - 1, place - 2)
                    p_place %= BPS
                    bv, qv, v_place = (bW, hs + 6, place - 3) if hs < 2 else (bT, hs - 2, place - 2)
                    v_place %= BPS
                    if isinstance(i, int) and i == 2 and hs == 0:
                        pe.wait_ge(a_lo, 8)
                    if hs == 1 and on(bQ):
                        pe.wait_ge(d_xt["B"], bQ + 1)
                        first_use(Q)
                        project(Q, xt_hi["B"], xt_lo["B"], p_q)
                    if hs == 3 and on(bW):
                        pe.wait_ge(d_ot, bW + 1)
                        project(O, ot_hi, ot_lo, p_wo)
                    if hs == 4 and on(bQ):
                        if on(bW):
                            pe.wait_ge(d_xt["C"], bW + 1)
                        else:
                            pe.wait_ge(d_qt, 2 * bQ + 2)
                        first_use(K)
                        project(K, xt_hi["B"], xt_lo["B"], p_k)
                    if on(bT):
                        if hs == 0:
                            pe.wait_ge(d_qt, 2 * bT + 2)
                            pe.wait_ge(a_kt, 2 * bT + 2)
                        if spare(i, hs - 1) if hs else isinstance(i, int) and spare(i - 1, 7):
                            need(pe, d_bias, 8 * bT + hs)
                        else:
                            need(pe, d_pt, 16 * bT + 2 * (hs - 1))
                        scores(bT, hs, (place - 2) % BPS)
                    if hs == 2 and on(bQ):
                        pe.wait_ge(d_qt, 2 * bQ + 1)
                        heads_t(1, p_qt)
                    if hs == 4 and on(bT) and spare(i, 3):
                        pe.wait_ge(d_pt, 16 * bT + 6)
                    if hs == 4 and spare(i, 3) and not on(bT) and on(bW):
                        pe.wait_ge(d_pt, 16 * NB)
                    if hs == 0 and on(bW) and isinstance(i, int) and spare(i - 1, 7):
                        pe.wait_ge(d_pt, 16 * bW + 14)
                    if hs < 4 and on(bA) and not early(i, hs):
                        if hs == 0:
                            pe.wait_ge(d_xt["A"], bA + 1)
                            need(pe, d_h["C"], 4 * (i - 4) + 4)
                            if isinstance(i, int) and i - 4 < 0:
                                need(pe, d_h["A"], 4 * bA)
                        else:
                            pe.wait_ge(d_h["A"], 4 * bA + c)
                        up("A", bA, c)
                    if hs >= 4 and on(bW):
                        if hs == 4:
                            pe.wait_ge(d_xt["C"], bW + 1)
                            pe.wait_ge(d_h["A"], 4 * last(i) + 4)
                            need(pe, d_h["C"], 4 * bW)
                        elif isinstance(i, int) and bW == NB - 1:
                            pe.wait_ge(d_h["C"], 4 * bW + c - 1)
                            pe.wait_ge(d_bias, 8 * NB)
                        else:
                            pe.wait_ge(d_h["C"], 4 * bW + c)
                        up("C", bW, c)
                    if hs < 4 and on(bE):
                        if hs == 0:
                            pe.wait_ge(d_hn["C"], 2 * bE + 1)
                            pe.wait_ge(d_ht["A"], 4 * last(i - 1) + 4)
                            need(pe, d_ht["C"], 4 * bE)
                        elif not (isinstance(i, int) and bE == NB - 1):
                            pe.wait_ge(d_ht["C"], 4 * bE + c)
                            pe.wait_ge(d_hn["C"], 2 * bE + 2)
                        if not (isinstance(i, int) and bE == NB - 1):
                            hidden_t("C", bE, c)
                        else:
                            if hs == 0:
                                hidden_t("C", bE, 0)
                                pe.wait_ge(d_hn["C"], 2 * bE + 2)
                            if c < 3:
                                pe.wait_ge(d_ht["C"], 4 * bE + c)
                                hidden_t("C", bE, c + 1)
                    if hs >= 4 and on(bA):
                        if hs == 4:
                            pe.wait_ge(d_hn["A"], 2 * bA + 1)
                            need(pe, d_ht["C"], 4 * (i - 4) + 4)
                            need(pe, d_ht["A"], 4 * bA)
                        else:
                            pe.wait_ge(d_ht["A"], 4 * bA + c)
                            pe.wait_ge(d_hn["A"], 2 * bA + 2)
                        hidden_t("A", bA, c)
                    if on(bv):
                        if qv == 0:
                            pe.wait_ge(g_v, bv + 1)
                        if qv % 2 == 0:
                            need(pe, d_on, 4 * bv + qv // 2)
                        prob_v(bv, qv, v_place)
                    if on(bp):
                        if spare(i, hs):
                            need(pe, d_pt, 16 * bp + 2 * qp)
                            if spare(i, hs) == "gu":
                                need(pe, d_h["A"], 4 * last(i if hs >= 4 else i - 1) + 4)
                                need(pe, d_h["C"], 4 * (i - 4) + 4)
                            else:
                                need(pe, d_ht["A"], 4 * last(i - 1) + 4)
                                need(pe, d_x1, last(i - 1) + 1)
                                need(pe, d_ht["C"], 4 * (i - 4 if hs >= 4 else i - 5) + 4)
                                need(pe, d_x3, i - 3 if hs >= 4 else i - 4)
                        else:
                            pe.wait_ge(d_bias, 8 * bT + hs + 1)
                        prob_t(bp, qp, pt_banks(i, hs), p_place)
                    if hs == 0 and on(bQ):
                        pe.wait_ge(d_xt["A"], last(i) + 1)
                        need(pe, d_v, bQ)
                        xt_piece("B", bQ)
                    if hs == 1 and on(bQ):
                        pe.wait_ge(d_q, bQ + 1)
                        heads_t(0, p_qt)
                    if hs == 2 and on(bW):
                        if on(bQ):
                            pe.wait_ge(d_qt, 2 * bQ + 2)
                        else:
                            pe.wait_ge(d_v, NB)
                            pe.wait_ge(d_xt["C"], bW)
                        pe.wait_ge(d_on, 4 * bW + 4)
                        for k in range(KD):
                            t = pe.transpose(ps_m[:, k * P:(k + 1) * P], o_norm[:, k * P:(k + 1) * P], id32[:, :])
                        t.then_inc(p_ot, 1)
                    if hs == 3 and on(bW):
                        xt_piece("C", bW)
                    if hs == 4 and on(bQ):
                        pe.wait_ge(d_k, bQ + 1)
                        heads_t(0, p_kt)
                    if hs == 5 and on(bQ):
                        pe.wait_ge(a_kt, 2 * bQ + 1)
                        heads_t(1, p_kt)
                    if hs == 6 and on(bL):
                        if on(bQ):
                            pe.wait_ge(a_kt, 2 * bQ + 2)
                        else:
                            need(pe, d_xt["A"], bL)
                        xt_piece("A", bL)
                    if hs == 7 and on(bQ):
                        if on(bL):
                            pe.wait_ge(d_xt["A"], bL + 1)
                        else:
                            pe.wait_ge(a_kt, 2 * bQ + 2)
                        first_use(V)
                        project(V, xt_hi["B"], xt_lo["B"], p_v, range(0, KD // 2))
                    if hs < 4 and on(bE):
                        if hs == 0:
                            pe.wait_ge(d_x1, last(i - 1) + 1)
                            need(pe, d_x3, bE)
                        down("C", bE, c)
                    if hs >= 4 and on(bA):
                        if hs == 4:
                            need(pe, d_x3, i - 3)
                            need(pe, d_x1, bA)
                        down("A", bA, c)
                    if hs == 7 and on(bQ):
                        project(V, xt_hi["B"], xt_lo["B"], p_v, range(KD // 2, KD))
                    if half_of_weight(i, hs, 0) is not None:
                        attention_weight(half_of_weight(i, hs, 0))

            all_iterations(pe, body, ternary_weights)
_INS=['L0_attn_x','L0_attn_Wq','L0_attn_Wk','L0_attn_Wv','L0_attn_Wo','L0_ffn_w_gate_up','L0_ffn_w_proj']
def kernel(**inputs):
    import numpy as _np
    import concourse.bacc as _bacc
    from concourse import mybir as _mybir
    from concourse.bass_utils import run_bass_kernel_spmd as _run
    nc=_bacc.Bacc("TRN2",target_bir_lowering=False,num_devices=1)
    arrays,args={},[]
    for name in _INS:
        a=_np.ascontiguousarray(inputs[name])
        arrays[f"in_{name}_dram"]=a
        args.append(nc.dram_tensor(f"in_{name}_dram",a.shape,_mybir.dt.from_np(a.dtype),kind="ExternalInput").ap())
    args.append(nc.dram_tensor("out_0_dram",(8,512,512),_mybir.dt.float32,kind="ExternalOutput").ap())
    macaron(nc,*args)
    r=_run(nc,[arrays],core_ids=[0])
    return r.results[0]["out_0_dram"]
```
